# Optimizing a Trainium2 kernel written in Bass

```python
import numpy as np
import jax
import jax.numpy as jnp

def _softmax(x, axis=-1):
    return jax.nn.softmax(x, axis=axis)
def _gelu(x):
    return jax.nn.gelu(x, approximate=True)
def _silu(x):
    return jax.nn.silu(x)
def _sigmoid(x):
    return jax.nn.sigmoid(x)
def _layernorm(x, axis=-1, eps=1e-5):
    m = jnp.mean(x, axis=axis, keepdims=True)
    v = jnp.var(x, axis=axis, keepdims=True)
    return (x - m) / jnp.sqrt(v + eps)
def _scatter_add(tgt, idx, src, axis=0):
    return tgt.at[idx].add(src)
def _segment_sum(src, seg, n):
    return jax.ops.segment_sum(src, seg, n)

kernel_name = 'mk_adj_preln_d4_adj_256_c9c8c5'

def setup_inputs(seed: int = 0):
    np.random.seed(seed)
    _w = jnp.asarray
    def _rec_inputs():
        import jax
        import jax.numpy as jnp
        _gk = jax.random.key(seed)
        x = 7.22e-05 + 1 * jax.random.normal(jax.random.fold_in(_gk, 1), (32, 512, 256), jnp.float32)
        _a = jax.random.bernoulli(jax.random.fold_in(_gk, 2), 0.0625, (32, 512, 512))
        _a = jnp.logical_or(_a, jnp.swapaxes(_a, -1, -2))
        _a = jnp.logical_or(_a, jnp.eye(512, dtype=bool))
        adj = _a.astype(jnp.int32)
        return x, adj
    x, adj = _rec_inputs()
    def _L0_gnn_setup():
        import jax, jax.numpy as jnp
        import numpy as np
        NEG_INF = -1000000000.0
        LEAKY_ALPHA = 0.2
        key = jax.random.key(seed)
        k1, k2, k3, k4 = jax.random.split(key, 4)
        B, N, Din, Dout = (16, 2048, 256, 256)
        h = jax.random.normal(k1, (B, N, Din), dtype=jnp.float32)
        adj = jax.random.randint(k2, (B, N, N), 0, 2, dtype=jnp.int32)
        W = jax.random.normal(k3, (Din, Dout), dtype=jnp.float32) * (1.0 / np.sqrt(Din))
        a = jax.random.normal(k4, (2 * Dout,), dtype=jnp.float32) * (1.0 / np.sqrt(2 * Dout))
        return {'h': h, 'adj': adj, 'W': W, 'a': a}
    _L0_gnn_all = _L0_gnn_setup()
    _L0_gnn_in = {k: v for k, v in _L0_gnn_all.items() if k in ('W', 'a', )}
    del _L0_gnn_all

    def _L1_gnn_setup():
        import math
        import jax, jax.numpy as jnp
        import numpy as np
        B, N, E, H = (1, 4096, 256, 8)
        D = E // H
        key = jax.random.key(seed)
        ks = jax.random.split(key, 10)
        s = 1.0 / math.sqrt(E)
        return {'x': jax.random.normal(ks[0], (B, N, E), dtype=jnp.float32), 'adjacency': jax.random.randint(ks[1], (B, N, N), 0, 2, dtype=jnp.int32), 'Wq': jax.random.normal(ks[2], (E, E), dtype=jnp.float32) * s, 'bq': jnp.zeros((E,), dtype=jnp.float32), 'Wk': jax.random.normal(ks[3], (E, E), dtype=jnp.float32) * s, 'bk': jnp.zeros((E,), dtype=jnp.float32), 'Wv': jax.random.normal(ks[4], (E, E), dtype=jnp.float32) * s, 'bv': jnp.zeros((E,), dtype=jnp.float32), 'Wo': jax.random.normal(ks[5], (E, E), dtype=jnp.float32) * s, 'bo': jnp.zeros((E,), dtype=jnp.float32)}
    _L1_gnn_all = _L1_gnn_setup()
    _L1_gnn_in = {k: v for k, v in _L1_gnn_all.items() if k in ('Wq', 'bq', 'Wk', 'bk', 'Wv', 'bv', 'Wo', 'bo', )}
    del _L1_gnn_all

    def _L2_gnn_setup():
        import jax, jax.numpy as jnp
        import numpy as np
        NEG_INF = -9000000000000000.0
        LEAKY_SLOPE = 0.2
        key = jax.random.key(seed)
        k1, k2, k3, k4, k5, k6 = jax.random.split(key, 6)
        B, N, D = (512, 200, 256)
        hidden = jax.random.normal(k1, (B, N, D), dtype=jnp.float32)
        adj = jax.random.randint(k2, (B, N, N), 0, 5, dtype=jnp.int32)
        a0 = jax.random.normal(k3, (D,), dtype=jnp.float32)
        a1 = jax.random.normal(k4, (D,), dtype=jnp.float32)
        a2 = jax.random.normal(k5, (D,), dtype=jnp.float32)
        a3 = jax.random.normal(k6, (D,), dtype=jnp.float32)
        return {'hidden': hidden, 'adj': adj, 'a0': a0, 'a1': a1, 'a2': a2, 'a3': a3}
    _L2_gnn_all = _L2_gnn_setup()
    _L2_gnn_in = {k: v for k, v in _L2_gnn_all.items() if k in ('a0', 'a1', 'a2', 'a3', )}
    del _L2_gnn_all

    def _L3_gnn_setup():
        import jax, jax.numpy as jnp
        import numpy as np
        NEG_INF = -1000000000.0
        LEAKY_SLOPE = 0.2
        key = jax.random.key(seed)
        k1, k2, k3, k4 = jax.random.split(key, 4)
        B, N, D_in, D_out = (8, 2048, 256, 256)
        x = jax.random.normal(k1, (B, N, D_in), dtype=jnp.float32)
        adj_matrix = jax.random.randint(k2, (B, N, N), 0, 2, dtype=jnp.int32)
        W = jax.random.normal(k3, (D_out, D_in), dtype=jnp.float32) / np.sqrt(D_in)
        a = jax.random.normal(k4, (1, 2 * D_out), dtype=jnp.float32) / np.sqrt(2 * D_out)
        return {'x': x, 'adj_matrix': adj_matrix, 'W': W, 'a': a}
    _L3_gnn_all = _L3_gnn_setup()
    _L3_gnn_in = {k: v for k, v in _L3_gnn_all.items() if k in ('W', 'a', )}
    del _L3_gnn_all

    return {
        "x": x,
        "adj": adj,
        "L0_gnn_W": _L0_gnn_in["W"],
        "L0_gnn_a": _L0_gnn_in["a"],
        "L1_gnn_Wq": _L1_gnn_in["Wq"],
        "L1_gnn_bq": _L1_gnn_in["bq"],
        "L1_gnn_Wk": _L1_gnn_in["Wk"],
        "L1_gnn_bk": _L1_gnn_in["bk"],
        "L1_gnn_Wv": _L1_gnn_in["Wv"],
        "L1_gnn_bv": _L1_gnn_in["bv"],
        "L1_gnn_Wo": _L1_gnn_in["Wo"],
        "L1_gnn_bo": _L1_gnn_in["bo"],
        "L2_gnn_a0": _L2_gnn_in["a0"],
        "L2_gnn_a1": _L2_gnn_in["a1"],
        "L2_gnn_a2": _L2_gnn_in["a2"],
        "L2_gnn_a3": _L2_gnn_in["a3"],
        "L3_gnn_W": _L3_gnn_in["W"],
        "L3_gnn_a": _L3_gnn_in["a"],
    }

def reference(x, adj, L0_gnn_W, L0_gnn_a, L1_gnn_Wq, L1_gnn_bq, L1_gnn_Wk, L1_gnn_bk, L1_gnn_Wv, L1_gnn_bv, L1_gnn_Wo, L1_gnn_bo, L2_gnn_a0, L2_gnn_a1, L2_gnn_a2, L2_gnn_a3, L3_gnn_W, L3_gnn_a):
    import jax
    import jax.numpy as jnp
    def _L0_gnn_ref(h, adj, W, a):
        import jax, jax.numpy as jnp
        import numpy as np
        NEG_INF = -1000000000.0
        LEAKY_ALPHA = 0.2
        Wh = jnp.einsum('bnd,de->bne', h, W)
        Dout = Wh.shape[-1]
        a1, a2 = (a[:Dout], a[Dout:])
        f_i = Wh @ a1
        f_j = Wh @ a2
        e = f_i[:, :, None] + f_j[:, None, :]
        e = jax.nn.leaky_relu(e, negative_slope=LEAKY_ALPHA)
        e = jnp.where(adj > 0, e, NEG_INF)
        alpha = jax.nn.softmax(e, axis=-1)
        out = jnp.einsum('bij,bjd->bid', alpha, Wh)
        return jax.nn.elu(out)

    def _L1_gnn_ref(x, adjacency, Wq, bq, Wk, bk, Wv, bv, Wo, bo):
        import math
        import jax, jax.numpy as jnp
        import numpy as np
        B, N, E, H = (1, 4096, 256, 8)
        D = E // H
        b, n, e = x.shape

        def heads(y):
            return y.reshape(b, n, H, D).transpose(0, 2, 1, 3)
        q = heads(x @ Wq.T + bq)
        k = heads(x @ Wk.T + bk)
        v = heads(x @ Wv.T + bv)
        scores = jnp.einsum('bhnd,bhmd->bhnm', q, k) / math.sqrt(D)
        mask = adjacency[:, None, :, :] == 0
        scores = jnp.where(mask, -jnp.inf, scores)
        w = jax.nn.softmax(scores, axis=-1)
        out = jnp.einsum('bhnm,bhmd->bhnd', w, v)
        out = out.transpose(0, 2, 1, 3).reshape(b, n, e)
        return out @ Wo.T + bo

    def _L2_gnn_ref(hidden, adj, a0, a1, a2, a3):
        import jax, jax.numpy as jnp
        import numpy as np
        NEG_INF = -9000000000000000.0
        LEAKY_SLOPE = 0.2
        def edge_score(a):
            s = jnp.einsum('bid,bjd->bij', hidden * a, hidden)
            return jax.nn.leaky_relu(s, LEAKY_SLOPE)
        e0, e1, e2, e3 = (edge_score(a0), edge_score(a1), edge_score(a2), edge_score(a3))
        alpha = jnp.where(adj == 1, e0, NEG_INF)
        alpha = jnp.where(adj == 2, e1, alpha)
        alpha = jnp.where(adj == 3, e2, alpha)
        alpha = jnp.where(adj == 4, e3, alpha)
        alpha = jax.nn.softmax(alpha, axis=-1)
        return jnp.matmul(alpha, hidden)

    def _L3_gnn_ref(x, adj_matrix, W, a):
        import jax, jax.numpy as jnp
        import numpy as np
        NEG_INF = -1000000000.0
        LEAKY_SLOPE = 0.2
        h = jnp.einsum('bnd,od->bno', x, W)
        D = h.shape[-1]
        a_left, a_right = (a[0, :D], a[0, D:])
        e = (h @ a_left)[:, :, None] + (h @ a_right)[:, None, :]
        e = jnp.where(e > 0, e, LEAKY_SLOPE * e)
        e = jnp.where(adj_matrix == 0, NEG_INF, e)
        alpha = jax.nn.softmax(e, axis=-1)
        return jnp.einsum('bij,bjd->bid', alpha, h)

    h = jnp.maximum(_layernorm(x, axis=-1), 0.0)
    x = x + _L0_gnn_ref(h, adj, L0_gnn_W, L0_gnn_a)
    h = jnp.maximum(_layernorm(x, axis=-1), 0.0)
    x = x + _L1_gnn_ref(h, adj, L1_gnn_Wq, L1_gnn_bq, L1_gnn_Wk, L1_gnn_bk, L1_gnn_Wv, L1_gnn_bv, L1_gnn_Wo, L1_gnn_bo)
    h = jnp.maximum(_layernorm(x, axis=-1), 0.0)
    x = x + _L2_gnn_ref(h, adj, L2_gnn_a0, L2_gnn_a1, L2_gnn_a2, L2_gnn_a3)
    h = jnp.maximum(_layernorm(x, axis=-1), 0.0)
    x = x + _L3_gnn_ref(h, adj, L3_gnn_W, L3_gnn_a)
    return x


_drawn_inputs = setup_inputs


def setup_inputs(seed=0):
    import zlib

    import numpy as np

    out = dict(_drawn_inputs(seed))
    spreads = {'L1_gnn_bq': (0.0, 0.8),
     'L1_gnn_bk': (0.0, 0.8),
     'L1_gnn_bv': (0.0, 0.1),
     'L1_gnn_bo': (0.0, 0.1)}
    factors = {'L3_gnn_a': 3.534}
    for name, (base, spread) in spreads.items():
        noise = np.random.default_rng([zlib.crc32(name.encode()), seed]).standard_normal(out[name].shape)
        drawn = base * np.exp(spread * noise) if base else spread * noise
        out[name] = jnp.asarray(drawn.astype(out[name].dtype))
    for name, factor in factors.items():
        out[name] = (out[name] * factor).astype(out[name].dtype)
    return out
```

```python
from contextlib import ExitStack

import concourse.bass as bass
from concourse import mybir

P = 128
SLOTS = 2
F32 = mybir.dt.float32
F16 = mybir.dt.float16
BF16 = mybir.dt.bfloat16
I16 = mybir.dt.int16
I32 = mybir.dt.int32
ALU = mybir.AluOpType
ACT = mybir.ActivationFunctionType
AX = mybir.AxisListType.X
MAX = bass.bass_isa.ReduceOp.max

EPS = 1e-5
SLOPE = 0.2
EDGE_FILL = -9e15
MASKED = -1e30
LOWEST = -3e38
EDGE_TYPES = 4
LAYERS = 4
GAT = (0, 3)


class Signal:

    def __init__(self, nc, ctx, name, per_round):
        self.sem = ctx.enter_context(nc.semaphore(name))
        self.per_round = per_round

    def wait(self, engine, rnd, k):
        engine.wait_ge(self.sem, rnd * self.per_round + k)

    def wait_second(self, engine, rnd, k, sem, value):
        second_wait(engine, sem, value, self.sem, rnd * self.per_round + k)


def second_wait(engine, sem, value, round_sem, round_value):
    if not isinstance(round_value, int):
        round_value = engine.to_reg(round_value)
    engine.wait_ge(sem, value)
    engine.wait_ge(round_sem, round_value)


class Bank:

    def __init__(self, nc, ctx, index, tensor):
        self.tensor = tensor
        self.filled = ctx.enter_context(nc.semaphore(f"bank{index}_filled"))
        self.emptied = ctx.enter_context(nc.semaphore(f"bank{index}_emptied"))
        self.per_round = 0


def gnn_stack_kernel(nc, x, adj, W0, a0_vec, Wq, bq, Wk, bk, Wv, bv, Wo, bo,
                     e0, e1, e2, e3, W3, a3_vec, out):
    B, N, D = x.shape
    H = 8
    HD = D // H
    NT = N // P
    DC = D // P
    ROUNDS = B // SLOTS
    HPG = P // HD
    GROUPS = H // HPG
    ITEMS = SLOTS * H
    QK_SCALE = float(HD) ** -0.5
    slots = range(SLOTS)

    x_nodes = x.rearrange("b (t p) d -> b p t d", p=P)
    out_nodes = out.rearrange("b (t p) d -> b p t d", p=P)
    adj_rows = adj.rearrange("b (t p) j -> b p t j", p=P)

    with ExitStack() as ctx:
        def sb(name, shape, dt):
            return ctx.enter_context(nc.sbuf_tensor(name, shape, dt))

        def sem(name):
            return ctx.enter_context(nc.semaphore(name))

        xs = sb("xs", [P, SLOTS, NT, D], F32)
        hs = sb("hs", [P, SLOTS, NT, D], F32)
        hT = sb("hT", [P, SLOTS, DC, N], F32)
        wh = sb("wh", [P, SLOTS, NT, D + 1], F32)
        pT = sb("pT", [P, HPG, NT, N], F32)
        ring = sb("ring", [P, 3, NT, N], F32)
        qs = sb("qs", [P, SLOTS, H, N], F16)
        ks = sb("ks", [P, SLOTS, H, N], F16)
        hi = sb("hi", [P, SLOTS, 2 * GROUPS, N], F16)
        lo = sb("lo", [P, SLOTS, 2 * GROUPS, N], F16)
        qf = sb("qf", [P, 2, N], F32)
        adj_in = sb("adj_in", [P, SLOTS, NT, N], I32)
        adjc = sb("adjc", [P, SLOTS, NT, N], BF16)
        adjT = sb("adjT", [P, SLOTS, NT, N], BF16)
        mask = sb("mask", [P, SLOTS, NT, N], BF16)

        w0 = sb("w0", [P, DC, D], F32)
        wqT = sb("wqT", [P, DC, D], F32)
        wkT = sb("wkT", [P, DC, D], F32)
        wvT = sb("wvT", [P, DC, D], F32)
        woT = sb("woT", [P, DC, D], F32)
        w3T = sb("w3T", [P, DC, D], F32)
        f_rep = sb("f_rep", [P, 2, DC, P], F32)
        f_col = sb("f_col", [P, 2, DC], F32)
        src_bc = sb("src_bc", [P, 2, D], F32)
        dst_bc = sb("dst_bc", [P, 2, D], F32)
        bv_bc = sb("bv_bc", [P, D], F32)
        bo_bc = sb("bo_bc", [P, D], F32)
        qk_bias = sb("qk_bias", [P, 2 * GROUPS], F32)
        edge_a = sb("edge_a", [P, EDGE_TYPES, DC], F32)
        ident = sb("ident", [P, P], F32)
        identb = sb("identb", [P, P], BF16)
        ones = sb("ones", [P, P], F32)
        minus_half = sb("minus_half", [P, NT], F32)

        stats = sb("stats", [P, SLOTS, NT, 6], F32)
        mv = sb("mv", [P, SLOTS, NT, 2], F32)
        veps = sb("veps", [P, SLOTS, NT], F32)
        negm = sb("negm", [P, SLOTS, NT], F32)
        rstd = sb("rstd", [P, SLOTS, NT], F32)
        shift = sb("shift", [P, SLOTS, NT], F32)
        g = sb("g", [P, SLOTS, NT], F32)
        gm = sb("gm", [P, SLOTS, 1], F32)
        gmax = sb("gmax", [P, SLOTS, 1], F32)
        ngmax = sb("ngmax", [P, SLOTS, 2], F32)
        bcol = sb("bcol", [P, SLOTS, NT], F32)
        dcol = sb("dcol", [P, SLOTS, NT], F32)
        rcp = sb("rcp", [P, SLOTS, NT], F32)
        rowmax = sb("rowmax", [P, SLOTS, NT, H], F32)
        negmax = sb("negmax", [P, SLOTS, H, NT], F32)
        den = sb("den", [P, SLOTS, NT, H], F32)
        edge_max = sb("edge_max", [P, SLOTS, NT], F32)
        edge_neg = sb("edge_neg", [P, SLOTS, NT], F32)
        edge_den = sb("edge_den", [P, SLOTS, NT], F32)

        def flat32(t, s):
            return t[:, s].rearrange("p h n -> p (h n)").bitcast(F32)

        z_lo = [flat32(ks, s).rearrange("p (r n) -> p r n", r=4)[:, 0] for s in slots]
        z_hi = [flat32(ks, s).rearrange("p (r n) -> p r n", r=4)[:, 1] for s in slots]
        elu_pos = [flat32(qs, s).rearrange("p (r t d) -> p r t d", r=2, t=NT)[:, 0] for s in slots]
        elu_exp = [flat32(qs, s).rearrange("p (r t d) -> p r t d", r=2, t=NT)[:, 1] for s in slots]
        edge = [flat32(qs, s).rearrange("p (t n) -> p t n", t=NT) for s in slots]
        ha = [flat32(ks, s).rearrange("p (r k n) -> p r k n", r=2, k=DC) for s in slots]

        banks = [Bank(nc, ctx, i, ctx.enter_context(nc.psum_tensor(f"bank{i}", [P, N], F32)))
                 for i in range(8)]
        RINGS = {"product": (0, 1, 2), "turned": (3, 4, 5), "mixed": (6, 7)}

        def attention_order():
            for i in range(ITEMS + 2):
                for t in range(NT):
                    if i < ITEMS:
                        yield "scores", i, t
                    if i >= 2:
                        yield "turn", i - 2, t
                if i >= 2 and (i - 2) % HPG == HPG - 1:
                    yield "mix", (i - 2) // HPG, 0
                if i >= 2 and (i - 2) % H == H - 1:
                    yield "project", (i - 2) // H, 0

        def fills():
            for s in slots:
                for j in range(NT // 2):
                    yield "turned", ("adj", s, j)
            for l in range(LAYERS):
                for s in slots:
                    for k in range(DC):
                        yield "turned", ("hT", l, s, k)
                if l in GAT:
                    for s in slots:
                        yield "mixed", ("f", l, s)
                        for j in range(NT // 2):
                            yield "product", ("wh", l, s, j)
                    for s in slots:
                        for t in range(NT):
                            yield "mixed", ("gat", l, s, t)
                if l == 1:
                    for s in slots:
                        for f in range(2 * GROUPS):
                            yield "product", ("qk", s, f)
                        for j in range(NT // 2):
                            yield "product", ("v", s, j)
                    for what, i, t in attention_order():
                        if what == "scores":
                            yield "product", ("scores", i, t)
                        if what == "turn":
                            yield "turned", ("probs", i, t)
                        if what == "mix":
                            yield "mixed", ("heads", i)
                        if what == "project":
                            for k in range(GROUPS):
                                yield "turned", ("rden", i, k)
                            for j in range(NT // 2):
                                yield "product", ("wo", i, j)
                if l == 2:
                    for c in range(EDGE_TYPES):
                        for s in slots:
                            for t in range(NT):
                                yield "product", ("edge", c, s, t)
                    for s in slots:
                        for j in range(NT):
                            yield "turned", ("eprobs", s, j)
                    for s in slots:
                        for t in range(NT):
                            yield "mixed", ("emix", s, t)

        place, used = {}, {name: 0 for name in RINGS}
        for name, key in fills():
            bank = banks[RINGS[name][used[name] % len(RINGS[name])]]
            used[name] += 1
            place[key] = (bank, bank.per_round)
            bank.per_round += 1

        def await_empty(pe, rnd, key):
            bank, nth = place[key]
            pe.wait_ge(bank.emptied, rnd * bank.per_round + nth + 1)
            return bank.tensor

        def await_filled(engine, rnd, key):
            bank, nth = place[key]
            engine.wait_ge(bank.filled, rnd * bank.per_round + nth + 1)
            return bank.tensor

        def await_chain_and_filled(engine, rnd, key, links):
            bank, nth = place[key]
            second_wait(engine, dve_chain, links, bank.filled, rnd * bank.per_round + nth + 1)
            return bank.tensor

        def await_read(engine, rnd, keys):
            last = {}
            for key in keys:
                bank, nth = place[key]
                last[id(bank)] = bank, nth
            for bank, nth in last.values():
                engine.wait_ge(bank.emptied, rnd * bank.per_round + nth + 2)

        def filled(key):
            return place[key][0].filled

        def emptied(key):
            return place[key][0].emptied

        def hT_keys(l, s):
            return [("hT", l, s, k) for k in range(DC)]

        consts_in = sem("consts_in")
        consts_made = sem("consts_made")
        consts_chain = sem("consts_chain")
        setup_filled = sem("setup_filled")
        setup_emptied = sem("setup_emptied")
        setup_done = sem("setup_done")
        x_in = [Signal(nc, ctx, f"x_in{s}", 16) for s in slots]
        adj_in_sem = [Signal(nc, ctx, f"adj_in_sem{s}", 16) for s in slots]
        stored = [Signal(nc, ctx, f"stored{s}", 16) for s in slots]
        adj_ready = Signal(nc, ctx, "adj_ready", SLOTS)
        adj_used = Signal(nc, ctx, "adj_used", SLOTS)
        var_ready = Signal(nc, ctx, "var_ready", LAYERS * SLOTS)
        norm_ready = Signal(nc, ctx, "norm_ready", LAYERS * SLOTS)
        h_ready = Signal(nc, ctx, "h_ready", LAYERS * SLOTS)
        gm_ready = Signal(nc, ctx, "gm_ready", 2 * SLOTS)
        gmax_ready = Signal(nc, ctx, "gmax_ready", 2 * SLOTS)
        rows_ready = Signal(nc, ctx, "rows_ready", 2 * SLOTS)
        outer_ready = Signal(nc, ctx, "outer_ready", 2 * SLOTS * NT)
        gat_probs = Signal(nc, ctx, "gat_probs", 2 * SLOTS)
        elu_out = Signal(nc, ctx, "elu_out", SLOTS)
        split_ready = Signal(nc, ctx, "split_ready", SLOTS * 2 * GROUPS)
        STACKED = 2 * GROUPS * HPG * 4 * 16
        stacked = [Signal(nc, ctx, f"stacked{s}", STACKED) for s in slots]
        v_ready = Signal(nc, ctx, "v_ready", SLOTS * NT // 2)
        bo_added = Signal(nc, ctx, "bo_added", SLOTS)
        scores_ready = Signal(nc, ctx, "scores_ready", ITEMS)
        probs_ready = Signal(nc, ctx, "probs_ready", ITEMS)
        rden_ready = Signal(nc, ctx, "rden_ready", SLOTS)
        heads_ready = Signal(nc, ctx, "heads_ready", SLOTS * GROUPS)
        edge_cleared = Signal(nc, ctx, "edge_cleared", SLOTS)
        ha_ready = Signal(nc, ctx, "ha_ready", EDGE_TYPES * SLOTS)
        edge_ready = Signal(nc, ctx, "edge_ready", SLOTS)
        edge_probs = Signal(nc, ctx, "edge_probs", SLOTS)
        dve_chain = sem("dve_chain")
        pool_chain = sem("pool_chain")
        CONST_DMAS = 5 + 1 + 4 + 2 + 2 * GROUPS + EDGE_TYPES * DC

        block = ctx.enter_context(nc.Block())

        @block.sync
        def _(sp):
            def const(dst, src):
                sp.dma_start(dst, src).then_inc(consts_in, 16)

            def row(v, lo_, size):
                return v[lo_:lo_ + size].rearrange("(o d) -> o d", o=1).partition_broadcast(P).squeeze(1)

            for k, w in enumerate((Wq, Wk, Wv, Wo, W3)):
                const(ring[:, k // 2, 2 * (k % 2)].rearrange("p (c d) -> p c d", c=DC),
                      w.rearrange("(c p) d -> p c d", p=P))
            const(w0[:, :, :], W0.rearrange("(c p) e -> p c e", p=P))
            const(src_bc[:, 0], row(a0_vec, 0, D))
            const(dst_bc[:, 0], row(a0_vec, D, D))
            const(src_bc[:, 1], row(a3_vec, 0, D))
            const(dst_bc[:, 1], row(a3_vec, D, D))
            const(bv_bc[:, :], row(bv, 0, D))
            const(bo_bc[:, :], row(bo, 0, D))
            for f, b in enumerate((bq, bk)):
                for gr in range(GROUPS):
                    const(qk_bias[:, f * GROUPS + gr:f * GROUPS + gr + 1],
                          b[gr * P:(gr + 1) * P].rearrange("(p o) -> p o", o=1))
            for c, a in enumerate((e0, e1, e2, e3)):
                for k in range(DC):
                    const(edge_a[:, c, k:k + 1], a[k * P:(k + 1) * P].rearrange("(p o) -> p o", o=1))
            for s in slots:
                sp.dma_start(xs[:, s], x_nodes[s]).then_inc(x_in[s].sem, 16)
                sp.dma_start(adj_in[:, s], adj_rows[s]).then_inc(adj_in_sem[s].sem, 16)

            def one_round(rnd, last):
                for s in slots:
                    for f in range(2 * GROUPS):
                        split_ready.wait(sp, rnd, s * 2 * GROUPS + f + 1)
                        keys, gr = divmod(f, GROUPS)
                        stack = (qs, ks)[keys]
                        for quarter, part in enumerate(((hi, lo, hi, lo), (hi, hi, lo, lo))[keys]):
                            for hh in range(HPG):
                                sp.dma_start(stack[HD * quarter:HD * (quarter + 1), s, gr * HPG + hh],
                                             part[HD * hh:HD * (hh + 1), s, f]).then_inc(stacked[s].sem, 16)
                if not last:
                    for s in slots:
                        adj_ready.wait(sp, rnd, s + 1)
                        sp.dma_start(adj_in[:, s], adj_rows[rnd * SLOTS + (SLOTS + s)]).then_inc(adj_in_sem[s].sem, 16)
                for s in slots:
                    await_read(sp, rnd, [("gat", LAYERS - 1, s, t) for t in range(NT)])
                    sp.dma_start(out_nodes[rnd * SLOTS + s], hs[:, s]).then_inc(stored[s].sem, 16)
                    if not last:
                        sp.dma_start(xs[:, s], x_nodes[rnd * SLOTS + (SLOTS + s)]).then_inc(x_in[s].sem, 16)

            if ROUNDS > 1:
                with sp.Fori(0, ROUNDS - 1) as rnd:
                    one_round(rnd, False)
            one_round(ROUNDS - 1, True)
            for s in slots:
                stored[s].wait(sp, ROUNDS - 1, 16 + 1)

        @block.gpsimd
        def _(pool):
            nc.gpsimd.memset(ident[:, :], 0.0).then_inc(consts_chain, 1)
            nc.gpsimd.memset(identb[:, :], 0.0).then_inc(consts_chain, 1)
            nc.gpsimd.memset(ones[:, :], 1.0).then_inc(consts_made, 1)
            nc.gpsimd.memset(minus_half[:, :], -0.5).then_inc(consts_made, 1)
            for s in slots:
                nc.gpsimd.memset(wh[:, s, :, D:D + 1], 1.0).then_inc(consts_made, 1)
            pool.wait_ge(consts_chain, 2)
            for m in (ident, identb):
                nc.gpsimd.affine_select(out=m[:, :], in_=m[:, :], compare_op=ALU.not_equal, fill=1.0, base=0,
                                        pattern=[[-1, P]], channel_multiplier=1).then_inc(consts_made, 1)
            pool.wait_ge(setup_done, 2)

            def clamp_adjacency(rnd):
                for s in slots:
                    adj_in_sem[s].wait_second(pool, rnd, 16, consts_chain, 2)
                    adj_used.wait_second(pool, rnd, s + 1, consts_chain, 2)
                    nc.gpsimd.tensor_scalar(adjc[:, s].rearrange("p t n -> p (t n)"),
                                            adj_in[:, s].rearrange("p t n -> p (t n)"),
                                            5.0, -1.0, ALU.min, ALU.max).then_inc(adj_ready.sem, 1)

            def normalise(rnd, l, s):
                nonlocal links
                var_ready.wait(pool, rnd, l * SLOTS + s + 1)
                nc.gpsimd.tensor_tensor(rstd[:, s], veps[:, s], minus_half[:, :], ALU.pow).then_inc(pool_chain, 1)
                links += 1
                pool.wait_ge(pool_chain, links)
                nc.gpsimd.tensor_tensor(shift[:, s], negm[:, s], rstd[:, s], ALU.mult).then_inc(norm_ready.sem, 1)

            def one_round(rnd, last):
                nonlocal links
                links = 0
                pool.sem_clear(pool_chain)
                for l in range(LAYERS):
                    for s in slots:
                        normalise(rnd, l, s)
                    if l in GAT:
                        for s in slots:
                            k = GAT.index(l) * SLOTS + s
                            gm_ready.wait_second(pool, rnd, k + 1, consts_chain, 2)
                            nc.gpsimd.partition_all_reduce(gmax[:, s], gm[:, s], P, MAX).then_inc(gmax_ready.sem, 1)
                    if l == 1:
                        for s in slots:
                            h_ready.wait(pool, rnd, l * SLOTS + s + 1)
                            nc.gpsimd.tensor_tensor(xs[:, s], xs[:, s], bo_bc[:, :].unsqueeze(1).to_broadcast([P, NT, D]),
                                                    ALU.add).then_inc(bo_added.sem, 1)
                        for s in slots:
                            bank, nth = place[("scores", s * H + H - 1, NT - 1)]
                            second_wait(pool, consts_chain, 2, bank.filled, rnd * bank.per_round + nth + 1)
                            nc.gpsimd.memset(edge[s], EDGE_FILL).then_inc(edge_cleared.sem, 1)
                if not last:
                    clamp_adjacency(rnd + 1)

            links = 0
            pool.sem_inc(adj_used.sem, SLOTS)
            clamp_adjacency(0)
            if ROUNDS > 1:
                with pool.Fori(0, ROUNDS - 1) as rnd:
                    one_round(rnd, False)
            one_round(ROUNDS - 1, True)

        @block.scalar
        def _(act):
            act.wait_ge(consts_in, CONST_DMAS * 16)
            nc.scalar.mul(qk_bias[:, 0:GROUPS], qk_bias[:, 0:GROUPS], QK_SCALE).then_inc(setup_done, 1)
            act.wait_ge(setup_done, 2)

            def copy_out(rnd, key, dst, src=lambda bank: bank[:, :]):
                bank = await_filled(act, rnd, key)
                nc.scalar.copy(dst, src(bank)).then_inc(emptied(key), 1)

            def features(rnd, l, s):
                norm_ready.wait(act, rnd, l * SLOTS + s + 1)
                if l == 0:
                    stored[s].wait(act, rnd, 1)
                for t in range(NT):
                    last = nc.scalar.activation(hs[:, s, t], xs[:, s, t], ACT.Relu, bias=shift[:, s, t:t + 1],
                                                scale=rstd[:, s, t:t + 1])
                last.then_inc(h_ready.sem, 1)

            def gat(rnd, l):
                gi = GAT.index(l)
                for s in slots:
                    for j in range(NT // 2):
                        copy_out(rnd, ("wh", l, s, j), wh[:, s, 2 * j:2 * j + 2, 0:D],
                                 lambda bank: bank[:, :].rearrange("p (a d) -> p a d", a=2))
                for s in slots:
                    await_read(act, rnd, [("f", l, s)])
                    nc.scalar.activation(bcol[:, s], g[:, s], ACT.Exp, bias=ngmax[:, s, 0:1])
                    nc.scalar.activation(dcol[:, s], g[:, s], ACT.Exp, bias=ngmax[:, s, 1:2], scale=SLOPE)
                    nc.scalar.activation(z_hi[s], z_hi[s], ACT.Exp, scale=SLOPE - 1.0)
                    nc.scalar.activation(z_lo[s], z_lo[s], ACT.Exp, scale=1.0 - SLOPE).then_inc(rows_ready.sem, 1)
                    rows_ready.wait(act, rnd, gi * SLOTS + s + 1)
                    for j in range(NT):
                        nc.scalar.activation(pT[:, s, j], z_lo[s], ACT.Copy,
                                             scale=bcol[:, s, j:j + 1]).then_inc(outer_ready.sem, 1)
                if l == 0:
                    for s in slots:
                        await_read(act, rnd, [("gat", l, s, t) for t in range(NT)])
                        nc.scalar.activation(elu_exp[s], elu_exp[s], ACT.Exp).then_inc(elu_out.sem, 1)

            def attention(rnd):
                for s in slots:
                    for f in range(2 * GROUPS):
                        key = ("qk", s, f)
                        bank = await_filled(act, rnd, key)
                        if s * 2 * GROUPS + f >= 2:
                            split_ready.wait(act, rnd, s * 2 * GROUPS + f - 1)
                        nc.scalar.activation(qf[:, f % 2], bank[:, :], ACT.Identity, bias=qk_bias[:, f:f + 1],
                                             scale=QK_SCALE if f < GROUPS else 1.0).then_inc(emptied(key), 1)
                for i in range(ITEMS + 2):
                    for t in range(NT):
                        if 1 <= i < ITEMS + 1:
                            s, h = divmod(i - 1, H)
                            if t == 0:
                                scores_ready.wait(act, rnd, i)
                            last = nc.scalar.activation(ring[:, (i - 1) % 3, t], ring[:, (i - 1) % 3, t], ACT.Exp,
                                                        bias=negmax[:, s, h, t:t + 1], accum_out=den[:, s, t, h:h + 1])
                            if t == NT - 1:
                                last.then_inc(probs_ready.sem, 1)
                        if i >= 2 and t % 2 == 1:
                            if (i - 2) // HPG:
                                await_filled(act, rnd, ("heads", (i - 2) // HPG - 1))
                            copy_out(rnd, ("probs", i - 2, t), pT[:, (i - 2) % HPG, t])
                    if i >= 2 and (i - 2) % HPG == HPG - 1:
                        s, gr = divmod((i - 2) // HPG, GROUPS)
                        copy_out(rnd, ("heads", s * GROUPS + gr), hT[:, s, gr])

            def edges(rnd):
                for c in range(EDGE_TYPES):
                    for s in slots:
                        if c == 0:
                            await_read(act, rnd, hT_keys(2, s))
                        if c >= 2:
                            await_filled(act, rnd, ("edge", c - 2, s, NT - 1))
                        for k in range(DC):
                            last = nc.scalar.activation(ha[s][:, c % 2, k], hT[:, s, k], ACT.Copy,
                                                        scale=edge_a[:, c, k:k + 1])
                        last.then_inc(ha_ready.sem, 1)
                for s in slots:
                    edge_ready.wait(act, rnd, s + 1)
                    for t in range(NT):
                        last = nc.scalar.activation(edge[s][:, t], edge[s][:, t], ACT.Exp, bias=edge_neg[:, s, t:t + 1],
                                                    accum_out=edge_den[:, s, t:t + 1])
                    last.then_inc(edge_probs.sem, 1)
                for s in slots:
                    for j in range(1, NT, 2):
                        copy_out(rnd, ("eprobs", s, j), pT[:, s, j])

            for s in slots:
                act.sem_inc(stored[s].sem, 1)
            with act.Fori(0, ROUNDS) as rnd:
                for s in slots:
                    for j in range(NT // 2):
                        copy_out(rnd, ("adj", s, j), adjT[:, s, 2 * j:2 * j + 2],
                                 lambda bank: bank[:, :].bitcast(BF16).rearrange("p (a n) -> p a n", a=2))
                for l in range(LAYERS):
                    for s in slots:
                        features(rnd, l, s)
                    for s in slots:
                        copy_out(rnd, ("hT", l, s, 1), hT[:, s, 1])
                    if l in GAT:
                        gat(rnd, l)
                    if l == 1:
                        attention(rnd)
                    if l == 2:
                        edges(rnd)

        @block.vector
        def _(dve):
            links = 0

            def link(instruction):
                nonlocal links
                links += 1
                instruction.then_inc(dve_chain, 1)
                dve.wait_ge(dve_chain, links)

            raw = [ring[:, k // 2, 2 * (k % 2)].rearrange("p (c d) -> p c d", c=DC) for k in range(5)]
            dve.wait_ge(consts_in, CONST_DMAS * 16)
            dve.wait_ge(consts_made, 4 + SLOTS)
            for k, dst in enumerate((wqT, wkT, wvT, woT, w3T)):
                for c in range(DC):
                    n = k * DC + c
                    dve.wait_ge(setup_filled, n + 1)
                    nc.vector.tensor_copy(dst[:, c], banks[n % 2].tensor[:, 0:D]).then_inc(setup_emptied, 1)
            dve.wait_ge(setup_emptied, 5 * DC)
            junk = hT[:, 0].rearrange("p k (a d) -> p (k a) d", a=2)
            for gi, w in enumerate((w0, w3T)):
                for c in range(DC):
                    last = nc.vector.tensor_tensor_reduce(out=junk[:, gi * DC + c], in0=w[:, c], in1=src_bc[:, gi],
                                                          scale=1.0, scalar=0.0, op0=ALU.mult, op1=ALU.add,
                                                          accum_out=f_col[:, gi, c:c + 1])
            link(last)
            for gi in range(2):
                for c in range(DC):
                    last = nc.vector.tensor_scalar(f_rep[:, gi, c], ones[:, :], f_col[:, gi, c:c + 1], None, ALU.mult)
            last.then_inc(setup_done, 1)

            def statistics(rnd, l, s):
                if l == 0:
                    x_in[s].wait(dve, rnd, 16)
                for t in range(NT):
                    last = nc.vector.bn_stats(stats[:, s, t], xs[:, s, t])
                link(last)
                for t in range(NT):
                    last = nc.vector.bn_aggr(mv[:, s, t], stats[:, s, t])
                link(last)
                nc.vector.tensor_scalar(negm[:, s], mv[:, s, :, 0], -1.0, None, ALU.mult)
                nc.vector.tensor_scalar(veps[:, s], mv[:, s, :, 1], EPS, None, ALU.add).then_inc(var_ready.sem, 1)

            def gat(rnd, l):
                gi = GAT.index(l)
                for s in slots:
                    await_read(dve, rnd, [("wh", l, s, j) for j in range(NT // 2)])
                    for t in range(NT):
                        last = nc.vector.tensor_tensor_reduce(out=elu_pos[s][:, t], in0=wh[:, s, t, 0:D],
                                                              in1=dst_bc[:, gi], scale=1.0, scalar=0.0, op0=ALU.mult,
                                                              op1=ALU.add, accum_out=g[:, s, t:t + 1])
                    link(last)
                    nc.vector.reduce_max(gm[:, s], g[:, s], AX).then_inc(gm_ready.sem, 1)
                for s in slots:
                    gmax_ready.wait(dve, rnd, gi * SLOTS + s + 1)
                    nc.vector.tensor_scalar(ngmax[:, s, 0:1], gmax[:, s], -1.0, None, ALU.mult)
                    nc.vector.tensor_scalar(ngmax[:, s, 1:2], gmax[:, s], -SLOPE, None, ALU.mult)
                    key = ("f", l, s)
                    bank = await_filled(dve, rnd, key)
                    nc.vector.tensor_scalar(z_lo[s], bank[:, :], gmax[:, s], 0.0, ALU.add, ALU.min)
                    nc.vector.tensor_scalar(z_hi[s], bank[:, :], gmax[:, s], 0.0, ALU.add,
                                            ALU.max).then_inc(emptied(key), 1)
                for s in slots:
                    rows_ready.wait(dve, rnd, gi * SLOTS + s + 1)
                    for j in range(NT):
                        outer_ready.wait(dve, rnd, (gi * SLOTS + s) * NT + j + 1)
                        last = nc.vector.scalar_tensor_tensor(out=pT[:, s, j], in0=z_hi[s], scalar=dcol[:, s, j:j + 1],
                                                              in1=pT[:, s, j], op0=ALU.mult, op1=ALU.max)
                    link(last)
                    if l == 0:
                        await_read(dve, rnd, [("adj", s, j) for j in range(NT // 2)])
                    for j in range(NT):
                        last = nc.vector.scalar_tensor_tensor(out=pT[:, s, j], in0=adjT[:, s, j], scalar=0.0,
                                                              in1=pT[:, s, j], op0=ALU.is_gt if l == 0 else ALU.not_equal,
                                                              op1=ALU.mult)
                    last.then_inc(gat_probs.sem, 1)
                for s in slots:
                    gat_residual(rnd, l, s)
                    if l == 0:
                        elu_out.wait(dve, rnd, s + 1)
                        link(nc.vector.tensor_tensor(xs[:, s], xs[:, s], elu_exp[s], ALU.add))
                        statistics(rnd, 1, s)

            def gat_residual(rnd, l, s):
                for t in range(NT):
                    key = ("gat", l, s, t)
                    bank = await_filled(dve, rnd, key)
                    link(nc.vector.reciprocal(rcp[:, s, t:t + 1], bank[:, D:D + 1]))
                    if l == 0:
                        nc.vector.tensor_scalar(elu_pos[s][:, t], bank[:, 0:D], rcp[:, s, t:t + 1], 0.0, ALU.mult, ALU.max)
                        nc.vector.tensor_scalar(elu_exp[s][:, t], bank[:, 0:D], rcp[:, s, t:t + 1], 0.0, ALU.mult,
                                                ALU.min).then_inc(emptied(key), 1)
                    else:
                        nc.vector.scalar_tensor_tensor(out=hs[:, s, t], in0=bank[:, 0:D], scalar=rcp[:, s, t:t + 1],
                                                       in1=xs[:, s, t], op0=ALU.mult, op1=ALU.add).then_inc(emptied(key), 1)
                if l == 0:
                    await_read(dve, rnd, [("gat", l, s, t) for t in range(NT)])
                    link(nc.vector.scalar_tensor_tensor(out=xs[:, s], in0=elu_pos[s], scalar=-1.0, in1=xs[:, s],
                                                        op0=ALU.add, op1=ALU.add))

            def attention(rnd):
                for s in slots:
                    adj_ready.wait(dve, rnd, s + 1)
                    link(nc.vector.tensor_scalar(mask[:, s], adjc[:, s], 0.0, MASKED, ALU.is_equal, ALU.mult))
                    for f in range(2 * GROUPS):
                        await_read(dve, rnd, [("qk", s, f)])
                        link(nc.vector.tensor_copy(hi[:, s, f], qf[:, f % 2]))
                        nc.vector.tensor_tensor(lo[:, s, f], qf[:, f % 2], hi[:, s, f],
                                                ALU.subtract).then_inc(split_ready.sem, 1)
                    for j in range(NT // 2):
                        key = ("v", s, j)
                        bank = await_filled(dve, rnd, key)
                        nc.vector.tensor_tensor(wh[:, s, 2 * j:2 * j + 2, 0:D],
                                                bank[:, :].rearrange("p (a d) -> p a d", a=2),
                                                bv_bc[:, :].unsqueeze(1).to_broadcast([P, 2, D]),
                                                ALU.add).then_inc(emptied(key), 1)
                masks_made = links
                for i in range(ITEMS + 2):
                    for t in range(NT):
                        if i < ITEMS:
                            s, h = divmod(i, H)
                            if t == 0 and i >= 3:
                                await_chain_and_filled(dve, rnd, ("probs", i - 3, NT - 1), masks_made)
                            key = ("scores", i, t)
                            bank = await_chain_and_filled(dve, rnd, key, masks_made)
                            last = nc.vector.tensor_tensor_reduce(out=ring[:, i % 3, t], in0=bank[:, :],
                                                                  in1=mask[:, s, t], scale=1.0, scalar=LOWEST,
                                                                  op0=ALU.add, op1=ALU.max,
                                                                  accum_out=rowmax[:, s, t, h:h + 1])
                            last.then_inc(emptied(key), 1)
                        if i >= 2 and t % 2 == 0:
                            if (i - 2) // HPG:
                                await_filled(dve, rnd, ("heads", (i - 2) // HPG - 1))
                            key = ("probs", i - 2, t)
                            bank = await_filled(dve, rnd, key)
                            nc.vector.tensor_copy(pT[:, (i - 2) % HPG, t], bank[:, :]).then_inc(emptied(key), 1)
                    if i < ITEMS:
                        await_read(dve, rnd, [("scores", i, t) for t in range(NT)])
                        nc.vector.tensor_scalar(negmax[:, s, h], rowmax[:, s, :, h], -1.0, None,
                                                ALU.mult).then_inc(scores_ready.sem, 1)
                    if i >= 2 and (i - 2) % H == H - 1:
                        project(rnd, (i - 2) // H)

            def project(rnd, s):
                probs_ready.wait(dve, rnd, (s + 1) * H)
                link(nc.vector.scalar_tensor_tensor(out=den[:, s], in0=rowmax[:, s], scalar=MASKED / 2, in1=den[:, s],
                                                    op0=ALU.is_ge, op1=ALU.mult))
                link(nc.vector.reciprocal(den[:, s], den[:, s]))
                nc.vector.tensor_copy(hs[:, s].rearrange("p t (h e) -> p t h e", h=H),
                                      den[:, s].unsqueeze(3).to_broadcast([P, NT, H, HD])).then_inc(rden_ready.sem, 1)
                for gr in range(GROUPS):
                    await_read(dve, rnd, [("heads", s * GROUPS + gr)])
                    key = ("rden", s, gr)
                    bank = await_filled(dve, rnd, key)
                    nc.vector.tensor_tensor(hT[:, s, gr], hT[:, s, gr], bank[:, :], ALU.mult).then_inc(emptied(key), 1)
                bo_added.wait(dve, rnd, s + 1)
                for j in range(NT // 2):
                    key = ("wo", s, j)
                    bank = await_filled(dve, rnd, key)
                    nc.vector.tensor_tensor(xs[:, s, 2 * j:2 * j + 2], xs[:, s, 2 * j:2 * j + 2],
                                            bank[:, :].rearrange("p (a d) -> p a d", a=2), ALU.add).then_inc(emptied(key), 1)
                await_read(dve, rnd, [("wo", s, j) for j in range(NT // 2)])
                statistics(rnd, 2, s)

            def edges(rnd):
                for c in range(EDGE_TYPES):
                    for s in slots:
                        link(nc.vector.tensor_scalar(mask[:, s].bitcast(I16), adjc[:, s], float(c + 1), None, ALU.is_equal))
                        if c == EDGE_TYPES - 1:
                            dve.sem_inc(adj_used.sem, 1)
                        if c == 0:
                            edge_cleared.wait(dve, rnd, s + 1)
                        for t in range(NT):
                            key = ("edge", c, s, t)
                            bank = await_chain_and_filled(dve, rnd, key, links)
                            nc.vector.copy_predicated(edge[s][:, t], mask[:, s, t].bitcast(I16),
                                                      bank[:, :]).then_inc(emptied(key), 1)
                for s in slots:
                    await_read(dve, rnd, [("edge", EDGE_TYPES - 1, s, t) for t in range(NT)])
                    link(nc.vector.reduce_max(edge_max[:, s], edge[s], AX))
                    link(nc.vector.scalar_tensor_tensor(out=edge_neg[:, s], in0=edge_max[:, s], scalar=SLOPE,
                                                        in1=edge_max[:, s], op0=ALU.mult, op1=ALU.max))
                    link(nc.vector.tensor_scalar(edge_neg[:, s], edge_neg[:, s], -1.0, None, ALU.mult))
                    nc.vector.scalar_tensor_tensor(out=edge[s], in0=edge[s], scalar=SLOPE, in1=edge[s],
                                                   op0=ALU.mult, op1=ALU.max).then_inc(edge_ready.sem, 1)
                for s in slots:
                    for j in range(0, NT, 2):
                        key = ("eprobs", s, j)
                        bank = await_filled(dve, rnd, key)
                        nc.vector.tensor_copy(pT[:, s, j], bank[:, :]).then_inc(emptied(key), 1)
                for s in slots:
                    edge_probs.wait(dve, rnd, s + 1)
                    link(nc.vector.reciprocal(rcp[:, s], edge_den[:, s]))
                    for t in range(NT):
                        key = ("emix", s, t)
                        bank = await_filled(dve, rnd, key)
                        nc.vector.scalar_tensor_tensor(out=xs[:, s, t], in0=bank[:, 0:D], scalar=rcp[:, s, t:t + 1],
                                                       in1=xs[:, s, t], op0=ALU.mult, op1=ALU.add).then_inc(emptied(key), 1)
                    await_read(dve, rnd, [("emix", s, t) for t in range(NT)])
                    statistics(rnd, 3, s)

            with dve.Fori(0, ROUNDS) as rnd:
                links = 0
                dve.sem_clear(dve_chain)
                for s in slots:
                    statistics(rnd, 0, s)
                for l in range(LAYERS):
                    for s in slots:
                        key = ("hT", l, s, 0)
                        bank = await_filled(dve, rnd, key)
                        nc.vector.tensor_copy(hT[:, s, 0], bank[:, :]).then_inc(emptied(key), 1)
                    if l in GAT:
                        gat(rnd, l)
                    if l == 1:
                        attention(rnd)
                    if l == 2:
                        edges(rnd)

        @block.tensor
        def _(pe):
            pe.wait_ge(consts_in, CONST_DMAS * 16)
            pe.wait_ge(consts_made, 4 + SLOTS)
            raw = [ring[:, k // 2, 2 * (k % 2)].rearrange("p (c d) -> p c d", c=DC) for k in range(5)]
            for k in range(5):
                for c in range(DC):
                    n = k * DC + c
                    if n >= 2:
                        pe.wait_ge(setup_emptied, n - 1)
                    for r in range(DC):
                        last = nc.tensor.transpose(banks[n % 2].tensor[:, r * P:(r + 1) * P],
                                                   raw[k][:, r, c * P:(c + 1) * P], ident[:, :])
                    last.then_inc(setup_filled, 1)
            pe.wait_ge(setup_done, 2)

            def turn(rnd, key, src):
                bank = await_empty(pe, rnd, key)
                for t in range(NT):
                    last = nc.tensor.transpose(bank[:, t * P:(t + 1) * P], src(t), ident[:, :])
                last.then_inc(filled(key), 1)

            def product(rnd, key, width, terms):
                bank = await_empty(pe, rnd, key)
                for a, sums in enumerate(terms):
                    for n, (lhsT, rhs) in enumerate(sums):
                        last = nc.tensor.matmul(bank[:, a * width:(a + 1) * width], lhsT, rhs,
                                                start=(n == 0), stop=(n == len(sums) - 1))
                last.then_inc(filled(key), 1)

            def project_nodes(rnd, key, s, j, w):
                product(rnd, key, D, [[(hT[:, s, k, t * P:(t + 1) * P], w[:, k]) for k in range(DC)]
                                      for t in (2 * j, 2 * j + 1)])

            def gat(rnd, l):
                gi = GAT.index(l)
                for s in slots:
                    await_read(pe, rnd, hT_keys(l, s))
                    product(rnd, ("f", l, s), N, [[(f_rep[:, gi, k], hT[:, s, k]) for k in range(DC)]])
                    for j in range(NT // 2):
                        project_nodes(rnd, ("wh", l, s, j), s, j, (w0, w3T)[gi])
                for s in slots:
                    gat_probs.wait(pe, rnd, gi * SLOTS + s + 1)
                    for t in range(NT):
                        product(rnd, ("gat", l, s, t), D + 1,
                                [[(pT[:, s, j, t * P:(t + 1) * P], wh[:, s, j]) for j in range(NT)]])

            def attention(rnd):
                for s in slots:
                    await_read(pe, rnd, hT_keys(1, s))
                    for f in range(2 * GROUPS):
                        w, gr = (wqT, wkT)[f // GROUPS], f % GROUPS
                        product(rnd, ("qk", s, f), N, [[(w[:, k, gr * P:(gr + 1) * P], hT[:, s, k]) for k in range(DC)]])
                    for j in range(NT // 2):
                        project_nodes(rnd, ("v", s, j), s, j, wvT)
                for what, i, t in attention_order():
                    if what == "scores":
                        s, h = divmod(i, H)
                        if h == 0 and t == 0:
                            stacked[s].wait(pe, rnd, STACKED)
                        product(rnd, ("scores", i, t), N, [[(qs[:, s, h, t * P:(t + 1) * P], ks[:, s, h])]])
                    if what == "turn":
                        if t == 0:
                            probs_ready.wait(pe, rnd, i + 1)
                        turn(rnd, ("probs", i, t), lambda q: ring[:, i % 3, q, t * P:(t + 1) * P])
                    if what == "mix":
                        s, gr = divmod(i, GROUPS)
                        key = ("heads", i)
                        bank = await_empty(pe, rnd, key)
                        await_read(pe, rnd, [("probs", i * HPG + hh, q) for hh in range(HPG) for q in range(NT)])
                        if gr == 0:
                            await_read(pe, rnd, [("v", s, j) for j in range(NT // 2)])
                        for q in range(NT):
                            for hh in range(HPG):
                                e = (gr * HPG + hh) * HD
                                last = nc.tensor.matmul(bank[hh * HD:(hh + 1) * HD, :], wh[:, s, q, e:e + HD], pT[:, hh, q],
                                                        start=(q == 0), stop=(q == NT - 1))
                        last.then_inc(filled(key), 1)
                    if what == "project":
                        rden_ready.wait(pe, rnd, i + 1)
                        for k in range(GROUPS):
                            turn(rnd, ("rden", i, k), lambda q: hs[:, i, q, k * P:(k + 1) * P])
                        await_read(pe, rnd, [("rden", i, k) for k in range(GROUPS)])
                        for j in range(NT // 2):
                            project_nodes(rnd, ("wo", i, j), i, j, woT)

            def edges(rnd):
                for c in range(EDGE_TYPES):
                    for s in slots:
                        if c == 0:
                            await_read(pe, rnd, hT_keys(2, s))
                        ha_ready.wait(pe, rnd, c * SLOTS + s + 1)
                        for t in range(NT):
                            product(rnd, ("edge", c, s, t), N,
                                    [[(ha[s][:, c % 2, k, t * P:(t + 1) * P], hT[:, s, k]) for k in range(DC)]])
                for s in slots:
                    edge_probs.wait(pe, rnd, s + 1)
                    for j in range(NT):
                        turn(rnd, ("eprobs", s, j), lambda q: edge[s][:, q, j * P:(j + 1) * P])
                for s in slots:
                    await_read(pe, rnd, [("eprobs", s, j) for j in range(NT)])
                    for t in range(NT):
                        product(rnd, ("emix", s, t), D,
                                [[(pT[:, s, j, t * P:(t + 1) * P], hs[:, s, j]) for j in range(NT)]])

            for bank in banks:
                pe.sem_inc(bank.emptied, 1)
            with pe.Fori(0, ROUNDS) as rnd:
                for s in slots:
                    adj_ready.wait(pe, rnd, s + 1)
                    for j in range(NT // 2):
                        key = ("adj", s, j)
                        bank = await_empty(pe, rnd, key)[:, :].bitcast(BF16)
                        for a in range(2):
                            for t in range(NT):
                                last = nc.tensor.transpose(bank[:, a * N + t * P:a * N + (t + 1) * P],
                                                           adjc[:, s, t, (2 * j + a) * P:(2 * j + a + 1) * P], identb[:, :])
                        last.then_inc(filled(key), 1)
                for l in range(LAYERS):
                    for s in slots:
                        h_ready.wait(pe, rnd, l * SLOTS + s + 1)
                        for k in range(DC):
                            turn(rnd, ("hT", l, s, k), lambda q: hs[:, s, q, k * P:(k + 1) * P])
                    if l in GAT:
                        gat(rnd, l)
                    if l == 1:
                        attention(rnd)
                    if l == 2:
                        edges(rnd)


_INS = ["x", "adj", "L0_gnn_W", "L0_gnn_a", "L1_gnn_Wq", "L1_gnn_bq", "L1_gnn_Wk", "L1_gnn_bk", "L1_gnn_Wv", "L1_gnn_bv",
        "L1_gnn_Wo", "L1_gnn_bo", "L2_gnn_a0", "L2_gnn_a1", "L2_gnn_a2", "L2_gnn_a3", "L3_gnn_W", "L3_gnn_a"]


def kernel(**inputs):
    import numpy as np
    import concourse.bacc as bacc
    from concourse.bass_utils import run_bass_kernel_spmd

    nc = bacc.Bacc("TRN2", target_bir_lowering=False, num_devices=1)
    arrays, args = {}, []
    for name in _INS:
        a = np.ascontiguousarray(inputs[name])
        if a.shape[:1] == (1,):
            a = a.reshape(-1)
        arrays[f"in_{name}"] = a
        args.append(nc.dram_tensor(f"in_{name}", a.shape, mybir.dt.from_np(a.dtype), kind="ExternalInput").ap())
    out = nc.dram_tensor("out", inputs["x"].shape, F32, kind="ExternalOutput").ap()
    gnn_stack_kernel(nc, *args, out)
    result = run_bass_kernel_spmd(nc, [arrays], core_ids=[0])
    return result.results[0]["out"]
```

```python
from contextlib import ExitStack

import concourse.bass as bass
from concourse import mybir

P = 128
F32 = mybir.dt.float32
F16 = mybir.dt.float16
BF16 = mybir.dt.bfloat16
I16 = mybir.dt.int16
I32 = mybir.dt.int32
ALU = mybir.AluOpType
ACT = mybir.ActivationFunctionType
AX = mybir.AxisListType.X
MAX = bass.bass_isa.ReduceOp.max

EPS = 1e-5
SLOPE = 0.2
EDGE_FILL = -9e15
MASKED = -1e30
LOWEST = -3e38
EDGE_TYPES = 4
H = 8
GROUPS = 2

FRONT, BACK = 0, 1
ORDER = [
    (BACK, "attend", 6), (BACK, "attend", 7), (FRONT, "norm", 0), (FRONT, "relu", 0), (FRONT, "convert", 0),
    (BACK, "mix", 6), (BACK, "mix", 7), (FRONT, "turn", 0), (FRONT, "project", 0), (BACK, "divide", 1),
    (BACK, "output", 0), (BACK, "norm", 2), (BACK, "relu", 2), (BACK, "turn", 2), (BACK, "edge_clear", 0),
    (BACK, "edge_scale", 0), (FRONT, "target", 0), (FRONT, "z", 0), (FRONT, "adjacency", 0), (BACK, "edge_mask", 0),
    (BACK, "edge", 0), (BACK, "edge", 1), (FRONT, "weigh", 0), (BACK, "edge", 2), (FRONT, "adj_apply", 0),
    (BACK, "edge", 3), (BACK, "edge_scale", 1), (BACK, "edge_mask", 1), (BACK, "edge", 4), (FRONT, "gather", 0),
    (FRONT, "gather", 1), (FRONT, "gather", 2), (FRONT, "gather", 3), (FRONT, "elu", 0), (FRONT, "norm", 1),
    (BACK, "edge", 5), (BACK, "edge", 6), (BACK, "edge", 7), (BACK, "edge_scale", 2), (BACK, "edge_mask", 2),
    (FRONT, "relu", 1), (BACK, "edge", 8), (BACK, "edge", 9), (FRONT, "turn", 1), (BACK, "edge", 10),
    (FRONT, "qk", 0), (FRONT, "qk", 1), (FRONT, "stack", 0), (FRONT, "qk", 2), (FRONT, "stack", 1), (FRONT, "qk", 3),
    (BACK, "edge", 11), (BACK, "edge_scale", 3), (FRONT, "masks", 0), (BACK, "edge_mask", 3), (FRONT, "bo", 0),
    (BACK, "edge", 12), (FRONT, "v", 0), (FRONT, "v", 1), (FRONT, "rowmax", 0), (FRONT, "rowmax", 1),
    (BACK, "edge", 13), (BACK, "edge", 14), (FRONT, "rowmax", 2), (BACK, "edge", 15), (FRONT, "copy_adjacency", 0),
    (FRONT, "rowmax", 3), (FRONT, "shift", 0), (FRONT, "rowmax", 4), (BACK, "edge_softmax", 0), (FRONT, "attend", 0),
    (FRONT, "attend", 1), (FRONT, "mix", 0), (BACK, "edge_exp", 0), (BACK, "edge_turn", 0), (FRONT, "rowmax", 5),
    (FRONT, "attend", 2), (FRONT, "mix", 1), (FRONT, "rowmax", 6), (BACK, "edge_gather", 0), (BACK, "edge_gather", 1),
    (BACK, "edge_gather", 2), (BACK, "edge_gather", 3), (FRONT, "attend", 3), (BACK, "norm", 3), (BACK, "relu", 3),
    (FRONT, "rowmax", 7), (FRONT, "mix", 2), (FRONT, "shift", 1), (BACK, "turn", 3), (BACK, "project", 3),
    (BACK, "target", 3), (FRONT, "attend", 4), (BACK, "z", 3), (FRONT, "mix", 3), (FRONT, "divide", 0),
    (FRONT, "attend", 5), (FRONT, "mix", 4), (BACK, "weigh", 3), (BACK, "adj_apply", 3), (FRONT, "copy_adjacency", 1),
    (FRONT, "mix", 5), (BACK, "gather", 12), (BACK, "gather", 13), (BACK, "gather", 14), (BACK, "gather", 15),
    (BACK, "store", 0),
]


class Signal:

    def __init__(self, nc, ctx, name, per_graph):
        self.sem = ctx.enter_context(nc.semaphore(name))
        self.per_graph = per_graph

    def wait(self, engine, graph, k):
        engine.wait_ge(self.sem, graph * self.per_graph + k)

    def wait_second(self, engine, graph, k, sem, value):
        second_wait(engine, sem, value, self.sem, graph * self.per_graph + k)


def second_wait(engine, sem, value, graph_sem, graph_value):
    if not isinstance(graph_value, int):
        graph_value = engine.to_reg(graph_value)
    engine.wait_ge(sem, value)
    engine.wait_ge(graph_sem, graph_value)


class Bank:

    def __init__(self, nc, ctx, index, tensor):
        self.tensor = tensor
        self.filled = ctx.enter_context(nc.semaphore(f"bank{index}_filled"))
        self.emptied = ctx.enter_context(nc.semaphore(f"bank{index}_emptied"))
        self.fills = [0, 0, 0]


FIRST, LOOP, LAST = range(3)


class Pass:

    def __init__(self, part, front, back, turn):
        self.part, self.front, self.back, self.turn = part, front, back, turn

    def steps(self):
        for half, name, arg in ORDER:
            if self.part == LOOP or half == (FRONT if self.part == FIRST else BACK):
                yield name, arg


def gnn_stack_kernel(nc, x, adj, W0, a0_vec, Wq, bq, Wk, bk, Wv, bv, Wo, bo,
                     e0, e1, e2, e3, W3, a3_vec, out):
    B, N, D = x.shape
    HD = D // H
    NT = N // P
    DC = D // P
    HPG = P // HD
    assert HPG * GROUPS == H
    QK_SCALE = float(HD) ** -0.5
    PROJECTIONS = 2 * GROUPS
    SPLIT_ROWS = 3 * HD
    ATTEND = GROUPS * NT

    x_nodes = x.rearrange("b (t p) d -> b p t d", p=P)
    out_nodes = out.rearrange("b (t p) d -> b p t d", p=P)
    adj_rows = adj.rearrange("b (t p) j -> b p t j", p=P)

    with ExitStack() as ctx:
        def sb(name, shape, dt):
            return ctx.enter_context(nc.sbuf_tensor(name, shape, dt))

        def sem(name):
            return ctx.enter_context(nc.semaphore(name))

        def signal(name, per_graph=1):
            return Signal(nc, ctx, name, per_graph)

        x_new = sb("x_new", [P, NT, D], F32)
        xs = [sb(f"xs{i}", [P, NT, D], F32) for i in range(2)]
        hs = [sb(f"hs{i}", [P, NT, D], F32) for i in range(2)]
        hT = [sb(f"hT{i}", [P, DC, N], F32) for i in range(2)]
        wh = [sb(f"wh{i}", [P, NT, D + 1], F32) for i in range(2)]
        adjc = [sb(f"adjc{i}", [P, NT, N], BF16) for i in range(2)]
        adjT = [sb(f"adjT{i}", [P, NT, N], BF16) for i in range(2)]
        mask = [sb(f"mask{i}", [P, NT, N], BF16) for i in range(2)]
        z_lo = [sb(f"z_lo{i}", [P, N], F32) for i in range(2)]
        z_hi = [sb(f"z_hi{i}", [P, N], F32) for i in range(2)]
        attend_probs = sb("attend_probs", [P, 2, HPG, N], F32)
        back_probs = sb("back_probs", [P, NT, N], F32)
        gat_pT = [attend_probs[:, 0], back_probs[:, :]]
        adj_in = sb("adj_in", [P, NT, N], I32)
        maskT = sb("maskT", [P, NT, N], BF16)
        elu_pos = sb("elu_pos", [P, NT, D], F32)
        elu_exp = sb("elu_exp", [P, NT, D], F32)
        qs_tiles = sb("qs", [P, H * NT, P], F16)
        qs = qs_tiles[:, :, :].rearrange("p (h t) n -> p h (t n)", t=NT)
        ks = sb("ks", [P, H, N], F16)
        hi = sb("hi", [P, PROJECTIONS, N], F16)
        lo = sb("lo", [P, PROJECTIONS, N], F16)
        qf = sb("qf", [P, 2, N], F32)
        rowmax = sb("rowmax", [P, H * NT], F32)
        shift_rows = sb("shift_rows", [HPG * NT, GROUPS, P], F16)
        heads = sb("heads", [P, GROUPS, N], F32)
        rden = sb("rden", [P, N], F32)
        edge = sb("edge", [P, NT, N], F32)
        ha = sb("ha", [P, 2, DC, N], F32)
        result = sb("result", [P, NT, D], F32)

        w0 = sb("w0", [P, DC, D], F32)
        wqT = sb("wqT", [P, DC, D], F32)
        wkT = sb("wkT", [P, DC, D], F32)
        wvT = sb("wvT", [P, DC, D], F32)
        woT = sb("woT", [P, DC, D], F32)
        w3T = sb("w3T", [P, DC, D], F32)
        f_rep = sb("f_rep", [P, 2, DC, P], F32)
        f_col = sb("f_col", [P, 2, DC], F32)
        src_bc = sb("src_bc", [P, 2, D], F32)
        dst_bc = sb("dst_bc", [P, 2, D], F32)
        bv_bc = sb("bv_bc", [P, D], F32)
        bo_bc = sb("bo_bc", [P, D], F32)
        qk_bias = sb("qk_bias", [P, PROJECTIONS], F32)
        edge_a = sb("edge_a", [P, EDGE_TYPES, DC], F32)
        parts = nc.dram_tensor("head_parts", (GROUPS, 2, 2, P, N), F16, kind="Internal").ap()

        ident = sb("ident", [P, P], F32)
        identb = sb("identb", [P, P], BF16)
        ones = sb("ones", [P, P], F32)
        minus_half = sb("minus_half", [P, NT], F32)

        stats = sb("stats", [P, 2, NT, 6], F32)
        mv = sb("mv", [P, 2, NT, 2], F32)
        veps = sb("veps", [P, 2, NT], F32)
        negm = sb("negm", [P, 2, NT], F32)
        rstd = sb("rstd", [P, 2, NT], F32)
        norm_bias = sb("norm_bias", [P, 2, NT], F32)
        g = sb("g", [P, 2, NT], F32)
        gm = sb("gm", [P, 2, 1], F32)
        gmax = sb("gmax", [P, 2, 1], F32)
        ngmax = sb("ngmax", [P, 2, 2], F32)
        bcol = sb("bcol", [P, 2, NT], F32)
        dcol = sb("dcol", [P, 2, NT], F32)
        rcp = sb("rcp", [P, 2, NT], F32)
        edge_max = sb("edge_max", [P, NT], F32)
        edge_neg = sb("edge_neg", [P, NT], F32)
        edge_den = sb("edge_den", [P, NT], F32)

        banks = [Bank(nc, ctx, i, ctx.enter_context(nc.psum_tensor(f"bank{i}", [P, N], F32)))
                 for i in range(8)]
        RINGS = {"front": (0, 1, 2), "mixed": (3,), "dens": (4,), "back": (5, 6, 7)}

        def fills(name, arg):
            if name == "turn":
                for k in range(DC):
                    yield "front" if arg < 2 else "back", ("hT", arg, k)
            if name == "project":
                ring = "front" if arg == 0 else "back"
                for j in range(NT // 2):
                    yield ring, ("wh", arg, j)
                yield ring, ("f", arg)
            if name == "adjacency":
                for j in range(NT // 2):
                    yield "front", ("adj", j)
            if name == "gather":
                l, t = divmod(arg, NT)
                yield "front" if l == 0 else "back", ("gat", l, t)
            if name in ("qk", "v"):
                yield "front", (name, arg)
            if name == "rowmax":
                for t in range(NT):
                    yield "front", ("scores", arg, t)
            if name == "shift":
                yield "front", ("shift", arg)
            if name == "attend":
                for hh in range(HPG):
                    yield "front", ("turned", arg, hh)
            if name == "mix" and arg % NT == NT - 1:
                yield "mixed", ("heads", arg // NT)
                yield "dens", ("dens", arg // NT)
            if name == "output":
                for j in range(NT // 2):
                    yield "back", ("wo", j)
            if name == "edge":
                yield "back", ("edge", arg // NT, arg % NT)
            if name == "edge_turn":
                for j in range(NT):
                    yield "back", ("eprobs", j)
            if name == "edge_gather":
                yield "back", ("emix", arg)

        place, used = {}, {name: 0 for name in RINGS}
        for part in (FIRST, LOOP, LAST):
            used = {name: 0 for name in RINGS}
            for name, arg in Pass(part, 0, 0, 0).steps():
                for ring, key in fills(name, arg):
                    bank = banks[RINGS[ring][used[ring] % len(RINGS[ring])]]
                    used[ring] += 1
                    place[part, key] = bank, bank.fills[part]
                    bank.fills[part] += 1

        def fills_before(now, key):
            bank, nth = place[now.part, key]
            if now.part == FIRST:
                return nth
            return now.turn * bank.fills[LOOP] + (bank.fills[FIRST] + nth)

        def await_empty(pe, now, key):
            bank = place[now.part, key][0]
            pe.wait_ge(bank.emptied, fills_before(now, key) + 1)
            return bank.tensor

        def await_filled(engine, now, key):
            bank = place[now.part, key][0]
            engine.wait_ge(bank.filled, fills_before(now, key) + 1)
            return bank.tensor

        def await_chain_and_filled(engine, now, key, links):
            bank = place[now.part, key][0]
            second_wait(engine, dve_chain, links, bank.filled, fills_before(now, key) + 1)
            return bank.tensor

        def await_read(engine, now, keys):
            last = {place[now.part, key][0]: key for key in keys}
            for bank, key in last.items():
                engine.wait_ge(bank.emptied, fills_before(now, key) + 2)

        def filled(now, key):
            return place[now.part, key][0].filled

        def emptied(now, key):
            return place[now.part, key][0].emptied

        def hT_keys(l):
            return [("hT", l, k) for k in range(DC)]

        def layer_input(l):
            return x_new if l == 0 else xs[l // 2]

        def half_of(l):
            return l // 2

        def graph_of(now, l):
            return now.back if l // 2 else now.front

        consts_in = sem("consts_in")
        consts_made = sem("consts_made")
        consts_chain = sem("consts_chain")
        setup_filled = sem("setup_filled")
        setup_emptied = sem("setup_emptied")
        setup_done = sem("setup_done")
        dve_chain = sem("dve_chain")
        pool_chain = sem("pool_chain")
        x_in = signal("x_in", 16)
        adj_landed = signal("adj_landed", 16)
        stored = signal("stored", 16)
        adj_ready = signal("adj_ready")
        adj_used = signal("adj_used")
        adjT_used = signal("adjT_used")
        x_used = signal("x_used")
        var_ready = [signal(f"var_ready{l}") for l in range(4)]
        norm_ready = [signal(f"norm_ready{l}") for l in range(4)]
        h_ready = [signal(f"h_ready{l}") for l in range(4)]
        gm_ready = {l: signal(f"gm_ready{l}") for l in (0, 3)}
        gmax_ready = {l: signal(f"gmax_ready{l}") for l in (0, 3)}
        rows_ready = {l: signal(f"rows_ready{l}") for l in (0, 3)}
        outer_ready = {l: signal(f"outer_ready{l}", NT) for l in (0, 3)}
        gat_probs = {l: signal(f"gat_probs{l}") for l in (0, 3)}
        elu_out = signal("elu_out")
        split_ready = signal("split_ready", PROJECTIONS)
        parted = [signal(f"parted{gr}", 2 * 16) for gr in range(GROUPS)]
        STACK_DMAS = 2 * 3
        stacked = [signal(f"stacked{gr}", STACK_DMAS * 16) for gr in range(GROUPS)]
        bo_added = signal("bo_added")
        heads_ready = signal("heads_ready", GROUPS)
        rowmax_ready = signal("rowmax_ready")
        shift_in = [signal(f"shift_in{gr}", 16) for gr in range(GROUPS)]
        masks_ready = signal("masks_ready")
        edge_cleared = signal("edge_cleared")
        ha_ready = signal("ha_ready", EDGE_TYPES)
        edge_ready = signal("edge_ready")
        edge_probs = signal("edge_probs")
        CONST_DMAS = 5 + 1 + 4 + 2 + 2 * GROUPS + EDGE_TYPES * DC
        POOL_CONSTS = 2 + 2 + 2 + 3

        def raw_weight(k):
            whole = (attend_probs[:, 0], attend_probs[:, 1], edge[:, :, :])[k // 2]
            return whole[:, 2 * (k % 2)].rearrange("p (c d) -> p c d", c=DC)


        def run(engine, one_pass):
            one_pass(Pass(FIRST, 0, None, 0))
            if B > 1:
                with engine.Fori(0, B - 1) as turn:
                    one_pass(Pass(LOOP, turn + 1, turn, turn))
            one_pass(Pass(LAST, None, B - 1, B - 1))

        block = ctx.enter_context(nc.Block())

        @block.sync
        def _(sp):
            def const(dst, src):
                sp.dma_start(dst, src).then_inc(consts_in, 16)

            def row(v, first, size):
                return v[first:first + size].rearrange("(o d) -> o d", o=1).partition_broadcast(P).squeeze(1)

            for k, w in enumerate((Wq, Wk, Wv, Wo, W3)):
                const(raw_weight(k), w.rearrange("(c p) d -> p c d", p=P))
            const(w0[:, :, :], W0.rearrange("(c p) e -> p c e", p=P))
            const(src_bc[:, 0], row(a0_vec, 0, D))
            const(dst_bc[:, 0], row(a0_vec, D, D))
            const(src_bc[:, 1], row(a3_vec, 0, D))
            const(dst_bc[:, 1], row(a3_vec, D, D))
            const(bv_bc[:, :], row(bv, 0, D))
            const(bo_bc[:, :], row(bo, 0, D))
            for f, b in enumerate((bq, bk)):
                for gr in range(GROUPS):
                    const(qk_bias[:, 2 * gr + f:2 * gr + f + 1],
                          b[gr * P:(gr + 1) * P].rearrange("(p o) -> p o", o=1))
            for c, a in enumerate((e0, e1, e2, e3)):
                for k in range(DC):
                    const(edge_a[:, c, k:k + 1], a[k * P:(k + 1) * P].rearrange("(p o) -> p o", o=1))

            def one_pass(now):
                if now.part != LAST:
                    if now.part != FIRST:
                        x_used.wait(sp, now.back, 1)
                    sp.dma_start(x_new[:, :, :], x_nodes[now.front]).then_inc(x_in.sem, 16)
                    if now.part != FIRST:
                        adj_ready.wait(sp, now.back, 1)
                    sp.dma_start(adj_in[:, :, :], adj_rows[now.front]).then_inc(adj_landed.sem, 16)
                for name, arg in now.steps():
                    if name == "stack":
                        gr, group = arg, slice(2 * arg, 2 * arg + 2)
                        split_ready.wait(sp, now.front, 2 * gr + 2)
                        for part, halves in enumerate((hi, lo)):
                            sp.dma_start(parts[gr, part].rearrange("f p n -> p f n"),
                                         halves[:, group]).then_inc(parted[gr].sem, 16)
                        parted[gr].wait(sp, now.front, 2 * 16)
                        for keys, stack in enumerate((qs, ks)):
                            for quarter, part in enumerate(((0, 1, 0), (0, 0, 1))[keys]):
                                sp.dma_start(stack[HD * quarter:HD * (quarter + 1), gr * HPG:(gr + 1) * HPG],
                                             parts[gr, part, keys].rearrange("(h p) n -> p h n", p=HD)
                                             ).then_inc(stacked[gr].sem, 16)
                    if name == "shift":
                        await_read(sp, now, [("shift", arg)])
                        sp.dma_start(qs_tiles[SPLIT_ROWS:SPLIT_ROWS + 1, arg * HPG * NT:(arg + 1) * HPG * NT],
                                     shift_rows[:, arg]).then_inc(shift_in[arg].sem, 16)

            run(sp, one_pass)
            stored.wait(sp, B - 1, 16 + 1)

        @block.gpsimd
        def _(pool):
            links = 0
            nc.gpsimd.memset(ident[:, :], 0.0).then_inc(consts_chain, 1)
            nc.gpsimd.memset(identb[:, :], 0.0).then_inc(consts_chain, 1)
            pool.wait_ge(consts_chain, 2)
            for m in (ident, identb):
                nc.gpsimd.affine_select(out=m[:, :], in_=m[:, :], compare_op=ALU.not_equal, fill=1.0, base=0,
                                        pattern=[[-1, P]], channel_multiplier=1).then_inc(consts_made, 1)
            nc.gpsimd.memset(ones[:, :], 1.0).then_inc(consts_made, 1)
            nc.gpsimd.memset(minus_half[:, :], -0.5).then_inc(consts_made, 1)
            for w in wh:
                nc.gpsimd.memset(w[:, :, D:D + 1], 1.0).then_inc(consts_made, 1)
            pool.wait_ge(consts_made, POOL_CONSTS - 3)
            nc.gpsimd.memset(ks[SPLIT_ROWS:P], 0.0).then_inc(consts_made, 1)
            nc.gpsimd.memset(qs_tiles[SPLIT_ROWS:P], 0.0).then_inc(consts_made, 1)
            pool.wait_ge(consts_made, POOL_CONSTS - 1)
            nc.gpsimd.memset(ks[SPLIT_ROWS:SPLIT_ROWS + 1], 1.0).then_inc(consts_made, 1)
            pool.wait_ge(consts_made, POOL_CONSTS)
            pool.sem_inc(adj_used.sem, 1)
            pool.sem_inc(stored.sem, 1)
            pool.wait_ge(setup_done, 2)

            def one_pass(now):
                nonlocal links
                links = 0
                pool.sem_clear(pool_chain)
                for name, arg in now.steps():
                    if name == "relu":
                        i, graph = half_of(arg), graph_of(now, arg)
                        var_ready[arg].wait(pool, graph, 1)
                        nc.gpsimd.tensor_tensor(rstd[:, i], veps[:, i], minus_half[:, :], ALU.pow).then_inc(pool_chain, 1)
                        links += 1
                        pool.wait_ge(pool_chain, links)
                        nc.gpsimd.tensor_tensor(norm_bias[:, i], negm[:, i], rstd[:, i],
                                                ALU.mult).then_inc(norm_ready[arg].sem, 1)
                    if name == "convert":
                        adj_landed.wait_second(pool, now.front, 16, consts_chain, 2)
                        adj_used.wait_second(pool, now.front, 1, consts_chain, 2)
                        nc.gpsimd.tensor_scalar(adjc[0][:, :, :].rearrange("p t n -> p (t n)"),
                                                adj_in[:, :, :].rearrange("p t n -> p (t n)"),
                                                5.0, -1.0, ALU.min, ALU.max).then_inc(adj_ready.sem, 1)
                    if name == "bo":
                        h_ready[1].wait(pool, now.front, 1)
                        nc.gpsimd.tensor_tensor(xs[0][:, :, :], xs[0][:, :, :],
                                                bo_bc[:, :].unsqueeze(1).to_broadcast([P, NT, D]),
                                                ALU.add).then_inc(bo_added.sem, 1)
                    if name == "edge_clear":
                        h_ready[2].wait_second(pool, now.back, 1, consts_chain, 2)
                        nc.gpsimd.memset(edge[:, :, :], EDGE_FILL).then_inc(edge_cleared.sem, 1)
                    if name == "target":
                        i, graph = half_of(arg), graph_of(now, arg)
                        gm_ready[arg].wait_second(pool, graph, 1, consts_chain, 2)
                        nc.gpsimd.partition_all_reduce(gmax[:, i], gm[:, i], P, MAX).then_inc(gmax_ready[arg].sem, 1)

            run(pool, one_pass)

        @block.scalar
        def _(act):
            act.wait_ge(consts_in, CONST_DMAS * 16)
            nc.scalar.mul(qk_bias[:, 0::2], qk_bias[:, 0::2], QK_SCALE).then_inc(setup_done, 1)
            act.wait_ge(setup_done, 2)

            def copy_out(now, key, dst, src=lambda bank: bank[:, :]):
                bank = await_filled(act, now, key)
                nc.scalar.copy(dst, src(bank)).then_inc(emptied(now, key), 1)

            def weigh(now, l):
                i, graph = half_of(l), graph_of(now, l)
                await_read(act, now, [("f", l)])
                nc.scalar.activation(bcol[:, i], g[:, i], ACT.Exp, bias=ngmax[:, i, 0:1])
                nc.scalar.activation(dcol[:, i], g[:, i], ACT.Exp, bias=ngmax[:, i, 1:2], scale=SLOPE)
                nc.scalar.activation(z_hi[i][:, :], z_hi[i][:, :], ACT.Exp, scale=SLOPE - 1.0)
                nc.scalar.activation(z_lo[i][:, :], z_lo[i][:, :], ACT.Exp, scale=1.0 - SLOPE).then_inc(rows_ready[l].sem, 1)
                rows_ready[l].wait(act, graph, 1)
                for j in range(NT):
                    nc.scalar.activation(gat_pT[i][:, j], z_lo[i][:, :], ACT.Copy,
                                         scale=bcol[:, i, j:j + 1]).then_inc(outer_ready[l].sem, 1)

            def one_pass(now):
                for name, arg in now.steps():
                    if name == "relu":
                        i, graph = half_of(arg), graph_of(now, arg)
                        norm_ready[arg].wait(act, graph, 1)
                        x = layer_input(arg)
                        for t in range(NT):
                            last = nc.scalar.activation(hs[i][:, t], x[:, t], ACT.Relu, bias=norm_bias[:, i, t:t + 1],
                                                        scale=rstd[:, i, t:t + 1])
                        last.then_inc(h_ready[arg].sem, 1)
                    if name == "turn":
                        copy_out(now, ("hT", arg, 1), hT[half_of(arg)][:, 1])
                    if name == "project":
                        for j in range(NT // 2):
                            copy_out(now, ("wh", arg, j), wh[half_of(arg)][:, 2 * j:2 * j + 2, 0:D],
                                     lambda bank: bank[:, :].rearrange("p (a d) -> p a d", a=2))
                    if name == "adjacency":
                        if now.part != FIRST:
                            adjT_used.wait(act, now.back, 1)
                        for j in range(NT // 2):
                            copy_out(now, ("adj", j), adjT[0][:, 2 * j:2 * j + 2],
                                     lambda bank: bank[:, :].bitcast(BF16).rearrange("p (a n) -> p a n", a=2))
                    if name == "weigh":
                        weigh(now, arg)
                    if name == "elu":
                        await_read(act, now, [("gat", 0, t) for t in range(NT)])
                        nc.scalar.activation(elu_exp[:, :, :], elu_exp[:, :, :], ACT.Exp).then_inc(elu_out.sem, 1)
                    if name == "qk":
                        f, key = arg, ("qk", arg)
                        bank = await_filled(act, now, key)
                        if f >= 2:
                            split_ready.wait(act, now.front, f - 1)
                        nc.scalar.activation(qf[:, f % 2], bank[:, :], ACT.Identity, bias=qk_bias[:, f:f + 1],
                                             scale=1.0 if f % 2 else QK_SCALE).then_inc(emptied(now, key), 1)
                    if name == "shift":
                        key = ("shift", arg)
                        bank = await_filled(act, now, key)
                        nc.scalar.mul(shift_rows[:, arg], bank[0:HPG * NT, 0:P], -1.0).then_inc(emptied(now, key), 1)
                    if name == "attend":
                        for hh in range(HPG):
                            key = ("turned", arg, hh)
                            bank = await_filled(act, now, key)
                            nc.scalar.activation(attend_probs[:, arg % 2, hh], bank[:, :],
                                                 ACT.Exp).then_inc(emptied(now, key), 1)
                    if name == "edge_scale":
                        if arg == 0:
                            await_read(act, now, hT_keys(2))
                        if arg >= 2:
                            await_filled(act, now, ("edge", arg - 2, NT - 1))
                        for k in range(DC):
                            last = nc.scalar.activation(ha[:, arg % 2, k], hT[1][:, k], ACT.Copy,
                                                        scale=edge_a[:, arg, k:k + 1])
                        last.then_inc(ha_ready.sem, 1)
                    if name == "store":
                        await_read(act, now, [("gat", 3, t) for t in range(NT)])
                        act.dma_start(out_nodes[now.back], result[:, :, :]).then_inc(stored.sem, 16)
                    if name == "edge_exp":
                        edge_ready.wait(act, now.back, 1)
                        for t in range(NT):
                            last = nc.scalar.activation(edge[:, t], edge[:, t], ACT.Exp, bias=edge_neg[:, t:t + 1],
                                                        accum_out=edge_den[:, t:t + 1])
                        last.then_inc(edge_probs.sem, 1)
                    if name == "edge_turn":
                        for j in range(1, NT, 2):
                            copy_out(now, ("eprobs", j), back_probs[:, j])

            run(act, one_pass)

        @block.vector
        def _(dve):
            links = 0

            def link(instruction):
                nonlocal links
                links += 1
                instruction.then_inc(dve_chain, 1)
                dve.wait_ge(dve_chain, links)

            dve.wait_ge(consts_in, CONST_DMAS * 16)
            dve.wait_ge(consts_made, POOL_CONSTS)
            for k, dst in enumerate((wqT, wkT, wvT, woT, w3T)):
                for c in range(DC):
                    n = k * DC + c
                    dve.wait_ge(setup_filled, n + 1)
                    nc.vector.tensor_copy(dst[:, c], banks[n % 2].tensor[:, 0:D]).then_inc(setup_emptied, 1)
            dve.wait_ge(setup_emptied, 5 * DC)
            for gi, w in enumerate((w0, w3T)):
                for c in range(DC):
                    last = nc.vector.tensor_tensor_reduce(out=elu_pos[:, gi * DC + c], in0=w[:, c], in1=src_bc[:, gi],
                                                          scale=1.0, scalar=0.0, op0=ALU.mult, op1=ALU.add,
                                                          accum_out=f_col[:, gi, c:c + 1])
            link(last)
            for gi in range(2):
                for c in range(DC):
                    last = nc.vector.tensor_scalar(f_rep[:, gi, c], ones[:, :], f_col[:, gi, c:c + 1], None, ALU.mult)
            last.then_inc(setup_done, 1)

            def statistics(now, l):
                i = half_of(l)
                for t in range(NT):
                    last = nc.vector.bn_stats(stats[:, i, t], layer_input(l)[:, t])
                link(last)
                for t in range(NT):
                    last = nc.vector.bn_aggr(mv[:, i, t], stats[:, i, t])
                link(last)
                nc.vector.tensor_scalar(negm[:, i], mv[:, i, :, 0], -1.0, None, ALU.mult)
                nc.vector.tensor_scalar(veps[:, i], mv[:, i, :, 1], EPS, None, ALU.add).then_inc(var_ready[l].sem, 1)

            def target_terms(now, l):
                i = half_of(l)
                await_read(dve, now, [("wh", l, j) for j in range(NT // 2)])
                for t in range(NT):
                    last = nc.vector.tensor_tensor_reduce(out=gat_pT[i][:, t, 0:D], in0=wh[i][:, t, 0:D],
                                                          in1=dst_bc[:, l // 3], scale=1.0, scalar=0.0, op0=ALU.mult,
                                                          op1=ALU.add, accum_out=g[:, i, t:t + 1])
                link(last)
                nc.vector.reduce_max(gm[:, i], g[:, i], AX).then_inc(gm_ready[l].sem, 1)

            def target_maxima(now, l):
                i = half_of(l)
                gmax_ready[l].wait(dve, graph_of(now, l), 1)
                nc.vector.tensor_scalar(ngmax[:, i, 0:1], gmax[:, i], -1.0, None, ALU.mult)
                nc.vector.tensor_scalar(ngmax[:, i, 1:2], gmax[:, i], -SLOPE, None, ALU.mult)
                key = ("f", l)
                bank = await_filled(dve, now, key)
                nc.vector.tensor_scalar(z_lo[i][:, :], bank[:, :], gmax[:, i], 0.0, ALU.add, ALU.min)
                nc.vector.tensor_scalar(z_hi[i][:, :], bank[:, :], gmax[:, i], 0.0, ALU.add,
                                        ALU.max).then_inc(emptied(now, key), 1)

            def weigh(now, l):
                i, graph = half_of(l), graph_of(now, l)
                pT = gat_pT[i]
                rows_ready[l].wait(dve, graph, 1)
                for j in range(NT):
                    outer_ready[l].wait(dve, graph, j + 1)
                    last = nc.vector.scalar_tensor_tensor(out=pT[:, j], in0=z_hi[i][:, :], scalar=dcol[:, i, j:j + 1],
                                                          in1=pT[:, j], op0=ALU.mult, op1=ALU.max)
                link(last)

            def adj_apply(now, l):
                i, pT = half_of(l), gat_pT[half_of(l)]
                if l == 0:
                    await_read(dve, now, [("adj", j) for j in range(NT // 2)])
                for j in range(NT):
                    last = nc.vector.scalar_tensor_tensor(out=pT[:, j], in0=adjT[i][:, j], scalar=0.0, in1=pT[:, j],
                                                          op0=ALU.is_gt if l == 0 else ALU.not_equal, op1=ALU.mult)
                last.then_inc(gat_probs[l].sem, 1)

            def gather(now, l, t):
                i = half_of(l)
                if l == 3 and t == 0:
                    stored.wait(dve, now.back, 1)
                key = ("gat", l, t)
                bank = await_filled(dve, now, key)
                link(nc.vector.reciprocal(rcp[:, i, t:t + 1], bank[:, D:D + 1]))
                if l == 0:
                    nc.vector.tensor_scalar(elu_pos[:, t], bank[:, 0:D], rcp[:, i, t:t + 1], 0.0, ALU.mult, ALU.max)
                    nc.vector.tensor_scalar(elu_exp[:, t], bank[:, 0:D], rcp[:, i, t:t + 1], 0.0, ALU.mult,
                                            ALU.min).then_inc(emptied(now, key), 1)
                else:
                    nc.vector.scalar_tensor_tensor(out=result[:, t], in0=bank[:, 0:D], scalar=rcp[:, i, t:t + 1],
                                                   in1=xs[1][:, t], op0=ALU.mult,
                                                   op1=ALU.add).then_inc(emptied(now, key), 1)

            def elu(now):
                await_read(dve, now, [("gat", 0, t) for t in range(NT)])
                link(nc.vector.scalar_tensor_tensor(out=xs[0][:, :, :], in0=elu_pos[:, :, :], scalar=-1.0,
                                                    in1=x_new[:, :, :], op0=ALU.add, op1=ALU.add))
                dve.sem_inc(x_used.sem, 1)
                elu_out.wait(dve, now.front, 1)
                link(nc.vector.tensor_tensor(xs[0][:, :, :], xs[0][:, :, :], elu_exp[:, :, :], ALU.add))

            def output(now):
                bo_added.wait(dve, now.back, 1)
                for j in range(NT // 2):
                    key = ("wo", j)
                    bank = await_filled(dve, now, key)
                    last = nc.vector.tensor_tensor(xs[1][:, 2 * j:2 * j + 2], xs[0][:, 2 * j:2 * j + 2],
                                                   bank[:, :].rearrange("p (a d) -> p a d", a=2),
                                                   ALU.add)
                    last.then_inc(emptied(now, key), 1)
                await_read(dve, now, [("wo", j) for j in range(NT // 2)])

            masks_made = edge_masks_made = 0

            def one_pass(now):
                nonlocal links, masks_made, edge_masks_made
                links = 0
                dve.sem_clear(dve_chain)
                for name, arg in now.steps():
                    if name == "norm":
                        if arg == 0:
                            x_in.wait(dve, now.front, 16)
                        statistics(now, arg)
                    if name == "turn":
                        i, key = half_of(arg), ("hT", arg, 0)
                        bank = await_filled(dve, now, key)
                        nc.vector.tensor_copy(hT[i][:, 0], bank[:, :]).then_inc(emptied(now, key), 1)
                    if name == "target":
                        target_terms(now, arg)
                    if name == "z":
                        target_maxima(now, arg)
                    if name == "weigh":
                        weigh(now, arg)
                    if name == "adj_apply":
                        adj_apply(now, arg)
                    if name == "gather":
                        gather(now, *divmod(arg, NT))
                    if name == "elu":
                        elu(now)
                    if name == "qk":
                        f = arg
                        await_read(dve, now, [("qk", f)])
                        link(nc.vector.tensor_copy(hi[:, f], qf[:, f % 2]))
                        nc.vector.tensor_tensor(lo[:, f], qf[:, f % 2], hi[:, f],
                                                ALU.subtract).then_inc(split_ready.sem, 1)
                    if name == "v":
                        key = ("v", arg)
                        bank = await_filled(dve, now, key)
                        nc.vector.tensor_tensor(wh[0][:, 2 * arg:2 * arg + 2, 0:D],
                                                bank[:, :].rearrange("p (a d) -> p a d", a=2),
                                                bv_bc[:, :].unsqueeze(1).to_broadcast([P, 2, D]),
                                                ALU.add).then_inc(emptied(now, key), 1)
                    if name == "masks":
                        adj_ready.wait(dve, now.front, 1)
                        nc.vector.tensor_scalar(mask[0][:, :, :], adjc[0][:, :, :], 0.0, MASKED, ALU.is_equal, ALU.mult)
                        link(nc.vector.tensor_scalar(maskT[:, :, :], adjT[0][:, :, :], 0.0, MASKED, ALU.is_equal,
                                                     ALU.mult))
                        masks_made = links
                        dve.sem_inc(masks_ready.sem, 1)
                    if name == "rowmax":
                        for t in range(NT):
                            key = ("scores", arg, t)
                            bank = await_chain_and_filled(dve, now, key, masks_made)
                            nc.vector.tensor_tensor_reduce(out=elu_exp[:, t].bitcast(BF16), in0=bank[:, :], in1=mask[0][:, t], scale=1.0,
                                                           scalar=LOWEST, op0=ALU.add, op1=ALU.max,
                                                           accum_out=rowmax[:, arg * NT + t:arg * NT + t + 1]
                                                           ).then_inc(emptied(now, key), 1)
                    if name == "divide":
                        gr = arg
                        key = ("dens", gr)
                        bank = await_filled(dve, now, key)
                        nc.vector.reciprocal(rden[:, :], bank[:, :]).then_inc(emptied(now, key), 1)
                        await_read(dve, now, [key])
                        key = ("heads", gr)
                        bank = await_filled(dve, now, key)
                        nc.vector.tensor_tensor(heads[:, gr], bank[:, :], rden[:, :],
                                                ALU.mult).then_inc(emptied(now, key), 1)
                        await_read(dve, now, [key])
                        dve.sem_inc(heads_ready.sem, 1)
                    if name == "output":
                        output(now)
                    if name == "copy_adjacency":
                        if arg == 0 and now.part != FIRST:
                            await_read(dve, now, [("edge", EDGE_TYPES - 1, 0)])
                        if arg == 1 and now.part != FIRST:
                            gat_probs[3].wait(dve, now.back, 1)
                        nc.vector.tensor_copy((adjc, adjT)[arg][1][:, :, :], (adjc, adjT)[arg][0][:, :, :]
                                              ).then_inc((adj_used, adjT_used)[arg].sem, 1)
                    if name == "edge_mask":
                        if arg == 0:
                            adj_used.wait(dve, now.back, 1 + 1)
                        if arg:
                            await_read(dve, now, [("edge", arg - 1, t) for t in range(NT)])
                        else:
                            edge_cleared.wait(dve, now.back, 1)
                        link(nc.vector.tensor_scalar(mask[1][:, :, :].bitcast(I16), adjc[1][:, :, :], float(arg + 1), None,
                                                     ALU.is_equal))
                        edge_masks_made = links
                    if name == "edge":
                        t, key = arg % NT, ("edge", arg // NT, arg % NT)
                        bank = await_chain_and_filled(dve, now, key, edge_masks_made)
                        nc.vector.copy_predicated(edge[:, t], mask[1][:, t].bitcast(I16),
                                                  bank[:, :]).then_inc(emptied(now, key), 1)
                    if name == "edge_softmax":
                        await_read(dve, now, [("edge", EDGE_TYPES - 1, t) for t in range(NT)])
                        link(nc.vector.reduce_max(edge_max[:, :], edge[:, :, :], AX))
                        link(nc.vector.scalar_tensor_tensor(out=edge_neg[:, :], in0=edge_max[:, :], scalar=SLOPE,
                                                            in1=edge_max[:, :], op0=ALU.mult, op1=ALU.max))
                        link(nc.vector.tensor_scalar(edge_neg[:, :], edge_neg[:, :], -1.0, None, ALU.mult))
                        nc.vector.scalar_tensor_tensor(out=edge[:, :, :], in0=edge[:, :, :], scalar=SLOPE,
                                                       in1=edge[:, :, :], op0=ALU.mult,
                                                       op1=ALU.max).then_inc(edge_ready.sem, 1)
                    if name == "edge_turn":
                        for j in range(0, NT, 2):
                            key = ("eprobs", j)
                            bank = await_filled(dve, now, key)
                            nc.vector.tensor_copy(back_probs[:, j], bank[:, :]).then_inc(emptied(now, key), 1)
                    if name == "edge_gather":
                        if arg == 0:
                            edge_probs.wait(dve, now.back, 1)
                            link(nc.vector.reciprocal(rcp[:, 1], edge_den[:, :]))
                        t, key = arg, ("emix", arg)
                        bank = await_filled(dve, now, key)
                        nc.vector.scalar_tensor_tensor(out=xs[1][:, t], in0=bank[:, 0:D], scalar=rcp[:, 1, t:t + 1],
                                                       in1=xs[1][:, t], op0=ALU.mult,
                                                       op1=ALU.add).then_inc(emptied(now, key), 1)
                        if arg == NT - 1:
                            await_read(dve, now, [("emix", t) for t in range(NT)])

            run(dve, one_pass)

        @block.tensor
        def _(pe):
            pe.wait_ge(consts_in, CONST_DMAS * 16)
            pe.wait_ge(consts_made, POOL_CONSTS)
            for k in range(5):
                for c in range(DC):
                    n = k * DC + c
                    if n >= 2:
                        pe.wait_ge(setup_emptied, n - 1)
                    for r in range(DC):
                        last = nc.tensor.transpose(banks[n % 2].tensor[:, r * P:(r + 1) * P],
                                                   raw_weight(k)[:, r, c * P:(c + 1) * P], ident[:, :])
                    last.then_inc(setup_filled, 1)
            pe.wait_ge(setup_done, 2)

            def turn(now, key, src):
                bank = await_empty(pe, now, key)
                for t in range(NT):
                    last = nc.tensor.transpose(bank[:, t * P:(t + 1) * P], src(t), ident[:, :])
                last.then_inc(filled(now, key), 1)

            def product(now, key, width, terms):
                bank = await_empty(pe, now, key)
                for a, sums in enumerate(terms):
                    for n, (lhsT, rhs) in enumerate(sums):
                        last = nc.tensor.matmul(bank[:, a * width:(a + 1) * width], lhsT, rhs,
                                                start=(n == 0), stop=(n == len(sums) - 1))
                last.then_inc(filled(now, key), 1)

            def project_nodes(now, key, nodesT, j, w):
                product(now, key, D, [[(nodesT[:, k, t * P:(t + 1) * P], w[:, k]) for k in range(DC)]
                                      for t in (2 * j, 2 * j + 1)])

            def mix(now, arg):
                gr, q = divmod(arg, NT)
                values = [("v", j) for j in range(NT // 2)] if arg == 0 else []
                await_read(pe, now, values + [("turned", arg, hh) for hh in range(HPG)])
                if arg == 0:
                    await_empty(pe, now, ("heads", 0))
                    await_empty(pe, now, ("dens", 0))
                elif q == 0:
                    await_read(pe, now, [("heads", gr - 1), ("dens", gr - 1)])
                for key, ring in ((("heads", gr), "mixed"), (("dens", gr), "dens")):
                    bank = banks[RINGS[ring][0]].tensor
                    for hh in range(HPG):
                        e = (gr * HPG + hh) * HD
                        weights = wh[0][:, q, e:e + HD] if key[0] == "heads" else ones[:, 0:HD]
                        last = nc.tensor.matmul(bank[hh * HD:(hh + 1) * HD, :], weights, attend_probs[:, arg % 2, hh],
                                                start=(q == 0), stop=(q == NT - 1))
                    if q == NT - 1:
                        last.then_inc(filled(now, key), 1)

            def one_pass(now):
                for name, arg in now.steps():
                    if name == "norm":
                        pass
                    if name == "turn":
                        i = half_of(arg)
                        h_ready[arg].wait(pe, graph_of(now, arg), 1)
                        for k in range(DC):
                            turn(now, ("hT", arg, k), lambda q: hs[i][:, q, k * P:(k + 1) * P])
                    if name == "project":
                        i = half_of(arg)
                        await_read(pe, now, hT_keys(arg))
                        for j in range(NT // 2):
                            project_nodes(now, ("wh", arg, j), hT[i], j, (w0, w3T)[i])
                        product(now, ("f", arg), N, [[(f_rep[:, i, k], hT[i][:, k]) for k in range(DC)]])
                    if name == "adjacency":
                        adj_ready.wait(pe, now.front, 1)
                        for j in range(NT // 2):
                            key = ("adj", j)
                            bank = await_empty(pe, now, key)[:, :].bitcast(BF16)
                            for a in range(2):
                                for t in range(NT):
                                    last = nc.tensor.transpose(bank[:, a * N + t * P:a * N + (t + 1) * P],
                                                               adjc[0][:, t, (2 * j + a) * P:(2 * j + a + 1) * P],
                                                               identb[:, :])
                            last.then_inc(filled(now, key), 1)
                    if name == "gather":
                        l, t = divmod(arg, NT)
                        i = half_of(l)
                        if t == 0:
                            gat_probs[l].wait(pe, graph_of(now, l), 1)
                        product(now, ("gat", l, t), D + 1,
                                [[(gat_pT[i][:, j, t * P:(t + 1) * P], wh[i][:, j]) for j in range(NT)]])
                    if name == "qk":
                        if arg == 0:
                            await_read(pe, now, hT_keys(1))
                        gr, keys = divmod(arg, 2)
                        product(now, ("qk", arg), N, [[((wqT, wkT)[keys][:, k, gr * P:(gr + 1) * P], hT[0][:, k])
                                                       for k in range(DC)]])
                    if name == "v":
                        project_nodes(now, ("v", arg), hT[0], arg, wvT)
                    if name == "rowmax":
                        if arg % HPG == 0:
                            stacked[arg // HPG].wait(pe, now.front, STACK_DMAS * 16)
                        for t in range(NT):
                            product(now, ("scores", arg, t), N,
                                    [[(qs[0:SPLIT_ROWS, arg, t * P:(t + 1) * P], ks[0:SPLIT_ROWS, arg])]])
                    if name == "shift":
                        await_read(pe, now, [("scores", (arg + 1) * HPG - 1, t) for t in range(NT)])
                        key = ("shift", arg)
                        bank = await_empty(pe, now, key)
                        nc.tensor.transpose(bank[0:HPG * NT, 0:P], rowmax[:, arg * HPG * NT:(arg + 1) * HPG * NT],
                                            ident[:, :]).then_inc(filled(now, key), 1)
                    if name == "attend":
                        if arg == 0:
                            masks_ready.wait(pe, now.front, 1)
                            pe.wait_ge(consts_made, POOL_CONSTS)
                        gr, q = divmod(arg, NT)
                        if q == 0:
                            shift_in[gr].wait(pe, now.front, 16)
                        for hh in range(HPG):
                            head = gr * HPG + hh
                            product(now, ("turned", arg, hh), N,
                                    [[(ks[:, head, q * P:(q + 1) * P], qs[:, head]), (identb[:, :], maskT[:, q])]])
                    if name == "mix":
                        mix(now, arg)
                    if name == "output":
                        heads_ready.wait(pe, now.back, GROUPS)
                        for j in range(NT // 2):
                            project_nodes(now, ("wo", j), heads, j, woT)
                    if name == "edge":
                        c, t = divmod(arg, NT)
                        if arg == 0:
                            await_read(pe, now, hT_keys(2))
                        if t == 0:
                            ha_ready.wait(pe, now.back, c + 1)
                        product(now, ("edge", c, t), N,
                                [[(ha[:, c % 2, k, t * P:(t + 1) * P], hT[1][:, k]) for k in range(DC)]])
                    if name == "edge_turn":
                        edge_probs.wait(pe, now.back, 1)
                        for j in range(NT):
                            turn(now, ("eprobs", j), lambda q: edge[:, q, j * P:(j + 1) * P])
                    if name == "edge_gather":
                        t = arg
                        if arg == 0:
                            await_read(pe, now, [("eprobs", j) for j in range(NT)])
                        product(now, ("emix", t), D,
                                [[(back_probs[:, j, t * P:(t + 1) * P], hs[1][:, j]) for j in range(NT)]])

            for bank in banks:
                pe.sem_inc(bank.emptied, 1)
            run(pe, one_pass)


_INS = ["x", "adj", "L0_gnn_W", "L0_gnn_a", "L1_gnn_Wq", "L1_gnn_bq", "L1_gnn_Wk", "L1_gnn_bk", "L1_gnn_Wv", "L1_gnn_bv",
        "L1_gnn_Wo", "L1_gnn_bo", "L2_gnn_a0", "L2_gnn_a1", "L2_gnn_a2", "L2_gnn_a3", "L3_gnn_W", "L3_gnn_a"]


def kernel(**inputs):
    import numpy as np
    import concourse.bacc as bacc
    from concourse.bass_utils import run_bass_kernel_spmd

    nc = bacc.Bacc("TRN2", target_bir_lowering=False, num_devices=1)
    arrays, args = {}, []
    for name in _INS:
        a = np.ascontiguousarray(inputs[name])
        if a.shape[:1] == (1,):
            a = a.reshape(-1)
        arrays[f"in_{name}"] = a
        args.append(nc.dram_tensor(f"in_{name}", a.shape, mybir.dt.from_np(a.dtype), kind="ExternalInput").ap())
    out = nc.dram_tensor("out", inputs["x"].shape, F32, kind="ExternalOutput").ap()
    gnn_stack_kernel(nc, *args, out)
    result = run_bass_kernel_spmd(nc, [arrays], core_ids=[0])
    return result.results[0]["out"]
```

```python
from contextlib import ExitStack

import concourse.bass as bass
from concourse import mybir

P = 128
F32 = mybir.dt.float32
F16 = mybir.dt.float16
BF16 = mybir.dt.bfloat16
I16 = mybir.dt.int16
I32 = mybir.dt.int32
ALU = mybir.AluOpType
ACT = mybir.ActivationFunctionType
AX = mybir.AxisListType.X
MAX = bass.bass_isa.ReduceOp.max

EPS = 1e-5
SLOPE = 0.2
EDGE_FILL = -9e15
MASKED = -1e30
LOWEST = -3e38
EDGE_TYPES = 4
H = 8
GROUPS = 2

FRONT, BACK, TAIL = 0, 1, 2
ORDER = [
    (FRONT, "norm", 0), (BACK, "attend", 3), (TAIL, "weigh", 3), (TAIL, "adj_apply", 3), (BACK, "mix", 3),
    (BACK, "divide", 0), (BACK, "attend", 4), (BACK, "attend", 5), (TAIL, "gather", 12), (FRONT, "relu", 0),
    (TAIL, "gather", 13), (BACK, "copy_adjacency", 1), (TAIL, "gather", 14), (BACK, "mix", 4), (FRONT, "turn", 0),
    (TAIL, "gather", 15), (BACK, "mix", 5), (FRONT, "convert", 0), (BACK, "attend", 6), (BACK, "attend", 7),
    (FRONT, "project", 0), (FRONT, "target", 0), (FRONT, "z", 0), (BACK, "count_types", 0), (BACK, "mix", 6),
    (BACK, "mix", 7), (BACK, "divide", 1), (FRONT, "adjacency", 0), (TAIL, "store", 0), (FRONT, "weigh", 0),
    (FRONT, "adj_apply", 0), (BACK, "output", 0), (BACK, "norm", 2), (FRONT, "gather", 0), (FRONT, "gather", 1),
    (FRONT, "gather", 2), (FRONT, "gather", 3), (BACK, "relu", 2), (BACK, "turn", 2), (BACK, "edge_scale", 0),
    (FRONT, "elu", 0), (BACK, "edge_clear", 0), (BACK, "edge_mask", 0), (FRONT, "norm", 1), (BACK, "edge", 0),
    (BACK, "edge", 1), (FRONT, "relu", 1), (FRONT, "stack", 0), (BACK, "edge", 2), (BACK, "edge", 3),
    (BACK, "edge_rest", 0), (FRONT, "turn", 1), (BACK, "edge_softmax", 0), (FRONT, "qk", 0), (FRONT, "qk", 1),
    (FRONT, "qk", 2), (FRONT, "v", 0), (BACK, "edge_exp", 0), (FRONT, "v", 1), (FRONT, "stack", 1),
    (BACK, "edge_turn", 0), (BACK, "edge_gather", 0), (FRONT, "masks", 0), (BACK, "edge_gather", 1),
    (BACK, "edge_gather", 2), (BACK, "edge_gather", 3), (BACK, "norm", 3), (FRONT, "qk", 3), (FRONT, "rowmax", 0),
    (BACK, "relu", 3), (FRONT, "bo", 0), (FRONT, "rowmax", 1), (FRONT, "rowmax", 2), (FRONT, "rowmax", 3),
    (FRONT, "rowmax", 4), (FRONT, "rowmax", 5), (BACK, "turn", 3), (FRONT, "rowmax", 6), (FRONT, "rowmax", 7),
    (BACK, "project", 3), (FRONT, "shift", 0), (FRONT, "rowmax", 8), (FRONT, "rowmax", 9), (FRONT, "attend", 0),
    (BACK, "target", 3), (FRONT, "rowmax", 10), (FRONT, "rowmax", 11), (BACK, "z", 3), (FRONT, "mix", 0),
    (FRONT, "attend", 1), (FRONT, "rowmax", 12), (FRONT, "rowmax", 13), (FRONT, "rowmax", 14), (FRONT, "mix", 1),
    (FRONT, "rowmax", 15), (FRONT, "copy_adjacency", 0), (FRONT, "attend", 2), (FRONT, "shift", 1), (FRONT, "mix", 2),
]


class Signal:

    def __init__(self, nc, ctx, name, per_graph):
        self.sem = ctx.enter_context(nc.semaphore(name))
        self.per_graph = per_graph

    def wait(self, engine, graph, k):
        engine.wait_ge(self.sem, graph * self.per_graph + k)

    def wait_second(self, engine, graph, k, sem, value):
        second_wait(engine, sem, value, self.sem, graph * self.per_graph + k)


def second_wait(engine, sem, value, graph_sem, graph_value):
    if not isinstance(graph_value, int):
        graph_value = engine.to_reg(graph_value)
    engine.wait_ge(sem, value)
    engine.wait_ge(graph_sem, graph_value)


class Bank:

    def __init__(self, nc, ctx, index, tensor):
        self.tensor = tensor
        self.filled = ctx.enter_context(nc.semaphore(f"bank{index}_filled"))
        self.emptied = ctx.enter_context(nc.semaphore(f"bank{index}_emptied"))
        self.fills = [0] * len(PARTS)


FIRST, SECOND, LOOP, BEFORE_LAST, LAST = range(5)
PARTS = ((FRONT,), (FRONT, BACK), (FRONT, BACK, TAIL), (BACK, TAIL), (TAIL,))


class Pass:

    def __init__(self, part, front, back, tail, turn=0):
        self.part, self.front, self.back, self.tail, self.turn = part, front, back, tail, turn
        self.graph = None

    def steps(self):
        for stage, name, arg in ORDER:
            if stage in PARTS[self.part]:
                self.graph = (self.front, self.back, self.tail)[stage]
                yield name, arg


def gnn_stack_kernel(nc, x, adj, W0, a0_vec, Wq, bq, Wk, bk, Wv, bv, Wo, bo,
                     e0, e1, e2, e3, W3, a3_vec, out):
    B, N, D = x.shape
    HD = D // H
    NT = N // P
    DC = D // P
    HPG = P // HD
    assert HPG * GROUPS == H and B > 2
    QK_SCALE = float(HD) ** -0.5
    PROJECTIONS = 2 * GROUPS
    SPLIT_ROWS = 3 * HD
    ATTEND = GROUPS * NT

    x_nodes = x.rearrange("b (t p) d -> b p t d", p=P)
    out_nodes = out.rearrange("b (t p) d -> b p t d", p=P)
    adj_rows = adj.rearrange("b (t p) j -> b p t j", p=P)

    with ExitStack() as ctx:
        def sb(name, shape, dt):
            return ctx.enter_context(nc.sbuf_tensor(name, shape, dt))

        def sem(name):
            return ctx.enter_context(nc.semaphore(name))

        def signal(name, per_graph=1):
            return Signal(nc, ctx, name, per_graph)

        x_new = sb("x_new", [P, NT, D], F32)
        xs = [sb(f"xs{i}", [P, NT, D], F32) for i in range(2)]
        hs = [sb(f"hs{i}", [P, NT, D], F32) for i in range(2)]
        hT = [sb(f"hT{i}", [P, DC, N], F32) for i in range(2)]
        wh = [sb(f"wh{i}", [P, NT, D + 1], F32) for i in range(2)]
        adjc = [sb(f"adjc{i}", [P, NT, N], BF16) for i in range(2)]
        adjT = [sb(f"adjT{i}", [P, NT, N], BF16) for i in range(2)]
        mask = [sb(f"mask{i}", [P, NT, N], BF16) for i in range(2)]
        z_lo = [sb(f"z_lo{i}", [P, N], F32) for i in range(2)]
        z_hi = [sb(f"z_hi{i}", [P, N], F32) for i in range(2)]
        attend_probs = sb("attend_probs", [P, 2, HPG, N], F32)
        back_probs = sb("back_probs", [P, NT, N], F32)
        front_probs = sb("front_probs", [P, NT, N], F32)
        gat_pT = [front_probs, back_probs]
        values = sb("values", [P, NT, D], F32)
        adj_in = sb("adj_in", [P, NT, N], I32)
        maskT = sb("maskT", [P, NT, N], BF16)
        elu_pos = sb("elu_pos", [P, NT, D], F32)
        elu_exp = sb("elu_exp", [P, NT, D], F32)
        qs_tiles = sb("qs", [P, H * NT, P], F16)
        qs = qs_tiles[:, :, :].rearrange("p (h t) n -> p h (t n)", t=NT)
        ks = sb("ks", [P, H, N], F16)
        hi = sb("hi", [P, PROJECTIONS, N], F16)
        lo = sb("lo", [P, PROJECTIONS, N], F16)
        rowmax = sb("rowmax", [P, H * NT], F32)
        shift_rows = sb("shift_rows", [HPG * NT, GROUPS, P], F16)
        heads = sb("heads", [P, GROUPS, N], F32)
        rden = sb("rden", [P, N], F32)
        edge = sb("edge", [P, NT, N], F32)
        ha = sb("ha", [P, 2, DC, N], F32)
        result = sb("result", [P, NT, D], F32)

        w0 = sb("w0", [P, DC, D], F32)
        wqT = sb("wqT", [P, DC, D], F32)
        wkT = sb("wkT", [P, DC, D], F32)
        wvT = sb("wvT", [P, DC, D], F32)
        woT = sb("woT", [P, DC, D], F32)
        w3T = sb("w3T", [P, DC, D], F32)
        f_rep = sb("f_rep", [P, 2, DC, P], F32)
        f_col = sb("f_col", [P, 2, DC], F32)
        src_bc = sb("src_bc", [P, 2, D], F32)
        dst_bc = sb("dst_bc", [P, 2, D], F32)
        bv_bc = sb("bv_bc", [P, D], F32)
        bo_bc = sb("bo_bc", [P, D], F32)
        qk_bias = sb("qk_bias", [P, PROJECTIONS], F32)
        edge_a = sb("edge_a", [P, EDGE_TYPES, DC], F32)
        parts = nc.dram_tensor("head_parts", (GROUPS, 2, 2, P, N), F16, kind="Internal").ap()

        ident = sb("ident", [P, P], F32)
        identb = sb("identb", [P, P], BF16)
        ones = sb("ones", [P, P], F32)
        minus_one = sb("minus_one", [P, 1], F32)
        minus_half = sb("minus_half", [P, NT], F32)

        stats = sb("stats", [P, 2, NT, 6], F32)
        mv = sb("mv", [P, 2, NT, 2], F32)
        veps = sb("veps", [P, 2, NT], F32)
        negm = sb("negm", [P, 2, NT], F32)
        rstd = sb("rstd", [P, 2, NT], F32)
        norm_bias = sb("norm_bias", [P, 2, NT], F32)
        g = sb("g", [P, 2, NT], F32)
        gm = sb("gm", [P, 2, 1], F32)
        gmax = sb("gmax", [P, 2, 1], F32)
        ngmax = sb("ngmax", [P, 2, 2], F32)
        bcol = sb("bcol", [P, 2, NT], F32)
        dcol = sb("dcol", [P, 2, NT], F32)
        rcp = sb("rcp", [P, 2, NT], F32)
        edge_max = sb("edge_max", [P, NT], F32)
        edge_neg = sb("edge_neg", [P, NT], F32)
        over_one = sb("over_one", [P, 1], F32)
        over_one_max = sb("over_one_max", [P, 1], F32)
        more_types = sb("more_types", [P, 1], I32)
        settled = sb("settled", [P, 1], F32)
        edge_den = sb("edge_den", [P, NT], F32)

        banks = [Bank(nc, ctx, i, ctx.enter_context(nc.psum_tensor(f"bank{i}", [P, N], F32)))
                 for i in range(8)]
        RINGS = {"front": (0, 1, 2), "mixed": (3,), "dens": (4,), "back": (5, 6, 7)}

        def half_head(arg):
            head, half = divmod(arg, 2)
            return [(head, t) for t in (2 * half, 2 * half + 1)]

        def fills(name, arg):
            if name == "turn":
                for k in range(DC):
                    yield "front" if arg < 2 else "back", ("hT", arg, k)
            if name == "project":
                ring = "front" if arg == 0 else "back"
                for j in range(NT // 2):
                    yield ring, ("wh", arg, j)
                yield ring, ("f", arg)
            if name == "adjacency":
                for j in range(NT // 2):
                    yield "front", ("adj", j)
            if name == "gather":
                l, t = divmod(arg, NT)
                yield "front" if l == 0 else "back", ("gat", l, t)
            if name in ("qk", "v"):
                yield "front", (name, arg)
            if name == "rowmax":
                for head, t in half_head(arg):
                    yield "front", ("scores", head, t)
            if name == "shift":
                yield "front", ("shift", arg)
            if name == "attend":
                for hh in range(HPG):
                    yield "front", ("turned", arg, hh)
            if name == "mix" and arg % NT == NT - 1:
                yield "mixed", ("heads", arg // NT)
                yield "dens", ("dens", arg // NT)
            if name == "output":
                for j in range(NT // 2):
                    yield "back", ("wo", j)
            if name == "edge":
                yield "back", ("edge", arg)
            if name == "edge_turn":
                for j in range(NT):
                    yield "back", ("eprobs", j)
            if name == "edge_gather":
                yield "back", ("emix", arg)

        place, used = {}, {name: 0 for name in RINGS}
        for part in range(len(PARTS)):
            used = {name: 0 for name in RINGS}
            for name, arg in Pass(part, 0, 0, 0).steps():
                for ring, key in fills(name, arg):
                    bank = banks[RINGS[ring][used[ring] % len(RINGS[ring])]]
                    used[ring] += 1
                    place[part, key] = bank, bank.fills[part]
                    bank.fills[part] += 1

        def fills_before(now, key):
            bank, nth = place[now.part, key]
            nth += sum(bank.fills[part] for part in range(now.part) if part != LOOP)
            return nth if now.part < LOOP else now.turn * bank.fills[LOOP] + nth

        def await_empty(pe, now, key):
            bank = place[now.part, key][0]
            pe.wait_ge(bank.emptied, fills_before(now, key) + 1)
            return bank.tensor

        def await_filled(engine, now, key):
            bank = place[now.part, key][0]
            engine.wait_ge(bank.filled, fills_before(now, key) + 1)
            return bank.tensor

        def await_chain_and_filled(engine, now, key, links):
            bank = place[now.part, key][0]
            second_wait(engine, dve_chain, links, bank.filled, fills_before(now, key) + 1)
            return bank.tensor

        def await_read(engine, now, keys):
            last = {place[now.part, key][0]: key for key in keys}
            for bank, key in last.items():
                engine.wait_ge(bank.emptied, fills_before(now, key) + 2)

        def filled(now, key):
            return place[now.part, key][0].filled

        def emptied(now, key):
            return place[now.part, key][0].emptied

        def hT_keys(l):
            return [("hT", l, k) for k in range(DC)]

        def rest_bank(n):
            return banks[RINGS["back"][n % len(RINGS["back"])]]

        def types_beyond_one(engine, now):
            more_types_ready.wait_second(engine, now.back, 1, consts_made, POOL_CONSTS)
            return engine.value_load(more_types[0:1, 0:1], min_val=0, max_val=EDGE_TYPES * NT * N)

        def layer_input(l):
            return x_new if l == 0 else xs[l // 2]

        def half_of(l):
            return l // 2

        consts_in = sem("consts_in")
        consts_made = sem("consts_made")
        consts_chain = sem("consts_chain")
        setup_filled = sem("setup_filled")
        setup_emptied = sem("setup_emptied")
        setup_done = sem("setup_done")
        dve_chain = sem("dve_chain")
        pool_chain = sem("pool_chain")
        x_in = signal("x_in", 16)
        adj_landed = signal("adj_landed", 16)
        stored = signal("stored", 16)
        adj_ready = signal("adj_ready")
        adj_used = signal("adj_used")
        adjT_used = signal("adjT_used")
        x_used = signal("x_used")
        var_ready = [signal(f"var_ready{l}") for l in range(4)]
        norm_ready = [signal(f"norm_ready{l}") for l in range(4)]
        h_ready = [signal(f"h_ready{l}") for l in range(4)]
        gm_ready = {l: signal(f"gm_ready{l}") for l in (0, 3)}
        gmax_ready = {l: signal(f"gmax_ready{l}") for l in (0, 3)}
        z_ready = {l: signal(f"z_ready{l}") for l in (0, 3)}
        rows_ready = {l: signal(f"rows_ready{l}") for l in (0, 3)}
        outer_ready = {l: signal(f"outer_ready{l}", NT) for l in (0, 3)}
        gat_probs = {l: signal(f"gat_probs{l}") for l in (0, 3)}
        elu_out = signal("elu_out")
        hi_ready = signal("hi_ready", PROJECTIONS)
        parted = [signal(f"parted{gr}", 2 * 16) for gr in range(GROUPS)]
        STACK_DMAS = 2 * 3
        stacked = [signal(f"stacked{gr}", STACK_DMAS * 16) for gr in range(GROUPS)]
        bo_added = signal("bo_added")
        heads_ready = signal("heads_ready", GROUPS)
        rowmax_ready = signal("rowmax_ready")
        shift_in = [signal(f"shift_in{gr}", 16) for gr in range(GROUPS)]
        attend_ready = signal("attend_ready")
        edge_cleared = signal("edge_cleared")
        ha_ready = signal("ha_ready")
        over_one_ready = signal("over_one_ready")
        more_types_ready = signal("more_types_ready")
        rest_scaled = sem("rest_scaled")
        rest_filled = sem("rest_filled")
        rest_read = sem("rest_read")
        rest_chain = sem("rest_chain")
        edge_ready = signal("edge_ready")
        edge_probs = signal("edge_probs")
        CONST_DMAS = 5 + 1 + 4 + 2 + 2 * GROUPS + EDGE_TYPES * DC
        POOL_CONSTS = 3 + 2 + 2 + 3

        def raw_weight(k):
            whole = (attend_probs[:, 0], attend_probs[:, 1], edge[:, :, :])[k // 2]
            return whole[:, 2 * (k % 2)].rearrange("p (c d) -> p c d", c=DC)


        def run(engine, one_pass):
            one_pass(Pass(FIRST, 0, None, None))
            one_pass(Pass(SECOND, 1, 0, None))
            with engine.Fori(0, B - 2) as turn:
                one_pass(Pass(LOOP, turn + 2, turn + 1, turn, turn))
            one_pass(Pass(BEFORE_LAST, None, B - 1, B - 2, B - 2))
            one_pass(Pass(LAST, None, None, B - 1, B - 2))

        block = ctx.enter_context(nc.Block())

        @block.sync
        def _(sp):
            def const(dst, src):
                sp.dma_start(dst, src).then_inc(consts_in, 16)

            def row(v, first, size):
                return v[first:first + size].rearrange("(o d) -> o d", o=1).partition_broadcast(P).squeeze(1)

            for k, w in enumerate((Wq, Wk, Wv, Wo, W3)):
                const(raw_weight(k), w.rearrange("(c p) d -> p c d", p=P))
            const(w0[:, :, :], W0.rearrange("(c p) e -> p c e", p=P))
            const(src_bc[:, 0], row(a0_vec, 0, D))
            const(dst_bc[:, 0], row(a0_vec, D, D))
            const(src_bc[:, 1], row(a3_vec, 0, D))
            const(dst_bc[:, 1], row(a3_vec, D, D))
            const(bv_bc[:, :], row(bv, 0, D))
            const(bo_bc[:, :], row(bo, 0, D))
            for f, b in enumerate((bq, bk)):
                for gr in range(GROUPS):
                    const(qk_bias[:, 2 * gr + f:2 * gr + f + 1],
                          b[gr * P:(gr + 1) * P].rearrange("(p o) -> p o", o=1))
            for c, a in enumerate((e0, e1, e2, e3)):
                for k in range(DC):
                    const(edge_a[:, c, k:k + 1], a[k * P:(k + 1) * P].rearrange("(p o) -> p o", o=1))

            def one_pass(now):
                if now.front is not None:
                    if now.part != FIRST:
                        x_used.wait(sp, now.back, 1)
                    sp.dma_start(x_new[:, :, :], x_nodes[now.front]).then_inc(x_in.sem, 16)
                    if now.part != FIRST:
                        adj_ready.wait(sp, now.back, 1)
                    sp.dma_start(adj_in[:, :, :], adj_rows[now.front]).then_inc(adj_landed.sem, 16)
                for name, arg in now.steps():
                    if name == "stack":
                        gr, group = arg, slice(2 * arg, 2 * arg + 2)
                        await_read(sp, now, [("qk", 2 * gr + 1)])
                        for part, halves in enumerate((hi, lo)):
                            sp.dma_start(parts[gr, part].rearrange("f p n -> p f n"),
                                         halves[:, group]).then_inc(parted[gr].sem, 16)
                        parted[gr].wait(sp, now.front, 2 * 16)
                        for keys, stack in enumerate((qs, ks)):
                            for quarter, part in enumerate(((0, 1, 0), (0, 0, 1))[keys]):
                                sp.dma_start(stack[HD * quarter:HD * (quarter + 1), gr * HPG:(gr + 1) * HPG],
                                             parts[gr, part, keys].rearrange("(h p) n -> p h n", p=HD)
                                             ).then_inc(stacked[gr].sem, 16)
                    if name == "shift":
                        await_read(sp, now, [("shift", arg)])
                        sp.dma_start(qs_tiles[SPLIT_ROWS:SPLIT_ROWS + 1, arg * HPG * NT:(arg + 1) * HPG * NT],
                                     shift_rows[:, arg]).then_inc(shift_in[arg].sem, 16)

            run(sp, one_pass)
            stored.wait(sp, B - 1, 16 + 1)

        @block.gpsimd
        def _(pool):
            links = 0
            nc.gpsimd.memset(ident[:, :], 0.0).then_inc(consts_chain, 1)
            nc.gpsimd.memset(identb[:, :], 0.0).then_inc(consts_chain, 1)
            pool.wait_ge(consts_chain, 2)
            for m in (ident, identb):
                nc.gpsimd.affine_select(out=m[:, :], in_=m[:, :], compare_op=ALU.not_equal, fill=1.0, base=0,
                                        pattern=[[-1, P]], channel_multiplier=1).then_inc(consts_made, 1)
            nc.gpsimd.memset(ones[:, :], 1.0).then_inc(consts_made, 1)
            nc.gpsimd.memset(minus_one[:, :], -1.0).then_inc(consts_made, 1)
            nc.gpsimd.memset(minus_half[:, :], -0.5).then_inc(consts_made, 1)
            for w in wh:
                nc.gpsimd.memset(w[:, :, D:D + 1], 1.0).then_inc(consts_made, 1)
            pool.wait_ge(consts_made, POOL_CONSTS - 3)
            nc.gpsimd.memset(ks[SPLIT_ROWS:P], 0.0).then_inc(consts_made, 1)
            nc.gpsimd.memset(qs_tiles[SPLIT_ROWS:P], 0.0).then_inc(consts_made, 1)
            pool.wait_ge(consts_made, POOL_CONSTS - 1)
            nc.gpsimd.memset(ks[SPLIT_ROWS:SPLIT_ROWS + 1], 1.0).then_inc(consts_made, 1)
            pool.wait_ge(consts_made, POOL_CONSTS)
            pool.sem_inc(adj_used.sem, 1)
            pool.sem_inc(stored.sem, 1)
            pool.wait_ge(setup_done, 2)

            def one_pass(now):
                nonlocal links
                links = 0
                pool.sem_clear(pool_chain)
                for name, arg in now.steps():
                    if name == "relu":
                        i, graph = half_of(arg), now.graph
                        var_ready[arg].wait(pool, graph, 1)
                        nc.gpsimd.tensor_tensor(rstd[:, i], veps[:, i], minus_half[:, :], ALU.pow).then_inc(pool_chain, 1)
                        links += 1
                        pool.wait_ge(pool_chain, links)
                        nc.gpsimd.tensor_tensor(norm_bias[:, i], negm[:, i], rstd[:, i],
                                                ALU.mult).then_inc(norm_ready[arg].sem, 1)
                    if name == "convert":
                        adj_landed.wait_second(pool, now.front, 16, consts_chain, 2)
                        adj_used.wait_second(pool, now.front, 1, consts_chain, 2)
                        nc.gpsimd.tensor_scalar(adjc[0][:, :, :].rearrange("p t n -> p (t n)"),
                                                adj_in[:, :, :].rearrange("p t n -> p (t n)"),
                                                5.0, -1.0, ALU.min, ALU.max).then_inc(adj_ready.sem, 1)
                    if name == "bo":
                        h_ready[1].wait(pool, now.front, 1)
                        nc.gpsimd.tensor_tensor(xs[0][:, :, :], xs[0][:, :, :],
                                                bo_bc[:, :].unsqueeze(1).to_broadcast([P, NT, D]),
                                                ALU.add).then_inc(bo_added.sem, 1)
                    if name == "edge_clear":
                        h_ready[2].wait_second(pool, now.back, 1, consts_chain, 2)
                        nc.gpsimd.memset(edge[:, :, :], EDGE_FILL).then_inc(edge_cleared.sem, 1)
                    if name == "count_types":
                        over_one_ready.wait_second(pool, now.back, 1, consts_chain, 2)
                        nc.gpsimd.partition_all_reduce(over_one_max[:, :], over_one[:, :], P, MAX).then_inc(pool_chain, 1)
                        links += 1
                        pool.wait_ge(pool_chain, links)
                        nc.gpsimd.tensor_copy(more_types[:, :], over_one_max[:, :]).then_inc(more_types_ready.sem, 1)
                    if name == "target":
                        i, graph = half_of(arg), now.graph
                        gm_ready[arg].wait_second(pool, graph, 1, consts_chain, 2)
                        nc.gpsimd.partition_all_reduce(gmax[:, i], gm[:, i], P, MAX).then_inc(gmax_ready[arg].sem, 1)

            run(pool, one_pass)

        @block.scalar
        def _(act):
            act.wait_ge(consts_in, CONST_DMAS * 16)
            nc.scalar.mul(qk_bias[:, 0::2], qk_bias[:, 0::2], QK_SCALE).then_inc(setup_done, 1)
            act.wait_ge(setup_done, 2)

            def copy_out(now, key, dst, src=lambda bank: bank[:, :]):
                bank = await_filled(act, now, key)
                nc.scalar.copy(dst, src(bank)).then_inc(emptied(now, key), 1)

            def scale_features(c):
                for k in range(DC):
                    last = nc.scalar.activation(ha[:, c % 2, k], hT[1][:, k], ACT.Copy, scale=edge_a[:, c, k:k + 1])
                return last

            def weigh(now, l):
                i, graph = half_of(l), now.graph
                z_ready[l].wait(act, graph, 1)
                nc.scalar.activation(bcol[:, i], g[:, i], ACT.Exp, bias=ngmax[:, i, 0:1])
                nc.scalar.activation(dcol[:, i], g[:, i], ACT.Exp, bias=ngmax[:, i, 1:2], scale=SLOPE)
                nc.scalar.activation(z_hi[i][:, :], z_hi[i][:, :], ACT.Exp, scale=SLOPE - 1.0)
                nc.scalar.activation(z_lo[i][:, :], z_lo[i][:, :], ACT.Exp, scale=1.0 - SLOPE).then_inc(rows_ready[l].sem, 1)
                rows_ready[l].wait(act, graph, 1)
                for j in range(NT):
                    nc.scalar.activation(gat_pT[i][:, j], z_lo[i][:, :], ACT.Copy,
                                         scale=bcol[:, i, j:j + 1]).then_inc(outer_ready[l].sem, 1)

            def one_pass(now):
                for name, arg in now.steps():
                    if name == "relu":
                        i, graph = half_of(arg), now.graph
                        norm_ready[arg].wait(act, graph, 1)
                        x = layer_input(arg)
                        for t in range(NT):
                            last = nc.scalar.activation(hs[i][:, t], x[:, t], ACT.Relu, bias=norm_bias[:, i, t:t + 1],
                                                        scale=rstd[:, i, t:t + 1])
                        last.then_inc(h_ready[arg].sem, 1)
                    if name == "turn":
                        copy_out(now, ("hT", arg, 1), hT[half_of(arg)][:, 1])
                    if name == "project":
                        for j in range(NT // 2):
                            copy_out(now, ("wh", arg, j), wh[half_of(arg)][:, 2 * j:2 * j + 2, 0:D],
                                     lambda bank: bank[:, :].rearrange("p (a d) -> p a d", a=2))
                    if name == "adjacency":
                        if now.part != FIRST:
                            adjT_used.wait(act, now.back, 1)
                        for j in range(NT // 2):
                            copy_out(now, ("adj", j), adjT[0][:, 2 * j:2 * j + 2],
                                     lambda bank: bank[:, :].bitcast(BF16).rearrange("p (a n) -> p a n", a=2))
                    if name == "weigh":
                        weigh(now, arg)
                    if name == "elu":
                        await_read(act, now, [("gat", 0, t) for t in range(NT)])
                        nc.scalar.activation(elu_exp[:, :, :], elu_exp[:, :, :], ACT.Exp).then_inc(elu_out.sem, 1)
                    if name == "qk":
                        bank = await_filled(act, now, ("qk", arg))
                        nc.scalar.activation(hi[:, arg], bank[:, :], ACT.Identity,
                                             bias=qk_bias[:, arg:arg + 1]).then_inc(hi_ready.sem, 1)
                    if name == "shift":
                        key = ("shift", arg)
                        bank = await_filled(act, now, key)
                        nc.scalar.mul(shift_rows[:, arg], bank[0:HPG * NT, 0:P], -1.0).then_inc(emptied(now, key), 1)
                    if name == "attend":
                        for hh in range(HPG):
                            key = ("turned", arg, hh)
                            bank = await_filled(act, now, key)
                            nc.scalar.activation(attend_probs[:, arg % 2, hh], bank[:, :],
                                                 ACT.Exp).then_inc(emptied(now, key), 1)
                    if name == "count_types":
                        adj_used.wait(act, now.back, 1 + 1)
                        nc.scalar.activation(ha[:, 1].rearrange("p c n -> p (c n)").bitcast(BF16)[:, 0:NT * N],
                                             adjc[1][:, :, :].rearrange("p t n -> p (t n)"), ACT.Relu, bias=minus_one[:, :],
                                             accum_out=over_one[:, :]).then_inc(over_one_ready.sem, 1)
                    if name == "edge_scale":
                        await_read(act, now, hT_keys(2))
                        scale_features(0).then_inc(ha_ready.sem, 1)
                    if name == "edge_rest":
                        with act.If(types_beyond_one(act, now) > 0):
                            for c in range(1, EDGE_TYPES):
                                if c == 2:
                                    await_filled(act, now, ("edge", NT - 1))
                                if c > 2:
                                    act.wait_ge(rest_filled, (c - 2) * NT)
                                scale_features(c).then_inc(rest_scaled, 1)
                    if name == "store":
                        await_read(act, now, [("gat", 3, t) for t in range(NT)])
                        act.dma_start(out_nodes[now.tail], result[:, :, :]).then_inc(stored.sem, 16)
                    if name == "edge_exp":
                        edge_ready.wait(act, now.back, 1)
                        for t in range(NT):
                            last = nc.scalar.activation(edge[:, t], edge[:, t], ACT.Exp, bias=edge_neg[:, t:t + 1],
                                                        accum_out=edge_den[:, t:t + 1])
                        last.then_inc(edge_probs.sem, 1)
                    if name == "edge_turn":
                        for j in range(1, NT, 2):
                            copy_out(now, ("eprobs", j), back_probs[:, j])

            run(act, one_pass)

        @block.vector
        def _(dve):
            links = 0

            def link(instruction):
                nonlocal links
                links += 1
                instruction.then_inc(dve_chain, 1)
                dve.wait_ge(dve_chain, links)

            dve.wait_ge(consts_in, CONST_DMAS * 16)
            dve.wait_ge(consts_made, POOL_CONSTS)
            for k, dst in enumerate((wqT, wkT, wvT, woT, w3T)):
                for c in range(DC):
                    n = k * DC + c
                    dve.wait_ge(setup_filled, n + 1)
                    nc.vector.tensor_scalar(dst[:, c], banks[n % 2].tensor[:, 0:D], QK_SCALE if dst is wqT else 1.0,
                                            None, ALU.mult).then_inc(setup_emptied, 1)
            dve.wait_ge(setup_emptied, 5 * DC)
            for gi, w in enumerate((w0, w3T)):
                for c in range(DC):
                    last = nc.vector.tensor_tensor_reduce(out=elu_pos[:, gi * DC + c], in0=w[:, c], in1=src_bc[:, gi],
                                                          scale=1.0, scalar=0.0, op0=ALU.mult, op1=ALU.add,
                                                          accum_out=f_col[:, gi, c:c + 1])
            link(last)
            for gi in range(2):
                for c in range(DC):
                    last = nc.vector.tensor_scalar(f_rep[:, gi, c], ones[:, :], f_col[:, gi, c:c + 1], None, ALU.mult)
            last.then_inc(setup_done, 1)

            def statistics(now, l):
                i = half_of(l)
                for t in range(NT):
                    last = nc.vector.bn_stats(stats[:, i, t], layer_input(l)[:, t])
                link(last)
                for t in range(NT):
                    last = nc.vector.bn_aggr(mv[:, i, t], stats[:, i, t])
                link(last)
                nc.vector.tensor_scalar(negm[:, i], mv[:, i, :, 0], -1.0, None, ALU.mult)
                nc.vector.tensor_scalar(veps[:, i], mv[:, i, :, 1], EPS, None, ALU.add).then_inc(var_ready[l].sem, 1)

            def target_terms(now, l):
                i = half_of(l)
                await_read(dve, now, [("wh", l, j) for j in range(NT // 2)])
                for t in range(NT):
                    last = nc.vector.tensor_tensor_reduce(out=gat_pT[i][:, t, 0:D], in0=wh[i][:, t, 0:D],
                                                          in1=dst_bc[:, l // 3], scale=1.0, scalar=0.0, op0=ALU.mult,
                                                          op1=ALU.add, accum_out=g[:, i, t:t + 1])
                link(last)
                nc.vector.reduce_max(gm[:, i], g[:, i], AX).then_inc(gm_ready[l].sem, 1)

            def target_maxima(now, l):
                i = half_of(l)
                gmax_ready[l].wait(dve, now.graph, 1)
                nc.vector.tensor_scalar(ngmax[:, i, 0:1], gmax[:, i], -1.0, None, ALU.mult)
                nc.vector.tensor_scalar(ngmax[:, i, 1:2], gmax[:, i], -SLOPE, None, ALU.mult)
                key = ("f", l)
                bank = await_filled(dve, now, key)
                nc.vector.tensor_scalar(z_lo[i][:, :], bank[:, :], gmax[:, i], 0.0, ALU.add, ALU.min)
                nc.vector.tensor_scalar(z_hi[i][:, :], bank[:, :], gmax[:, i], 0.0, ALU.add,
                                        ALU.max).then_inc(emptied(now, key), 1)
                await_read(dve, now, [key])
                dve.sem_inc(z_ready[l].sem, 1)

            def weigh(now, l):
                i, graph = half_of(l), now.graph
                pT = gat_pT[i]
                rows_ready[l].wait(dve, graph, 1)
                for j in range(NT):
                    outer_ready[l].wait(dve, graph, j + 1)
                    last = nc.vector.scalar_tensor_tensor(out=pT[:, j], in0=z_hi[i][:, :], scalar=dcol[:, i, j:j + 1],
                                                          in1=pT[:, j], op0=ALU.mult, op1=ALU.max)
                link(last)

            def type_mask(c):
                return nc.vector.tensor_scalar(mask[1][:, :, :].bitcast(I16), adjc[1][:, :, :], float(c + 1), None,
                                               ALU.is_equal)

            def take_scores(t, bank):
                return nc.vector.copy_predicated(edge[:, t], mask[1][:, t].bitcast(I16), bank[:, :])

            def adj_apply(now, l):
                i, pT = half_of(l), gat_pT[half_of(l)]
                if l == 0:
                    await_read(dve, now, [("adj", j) for j in range(NT // 2)])
                for j in range(NT):
                    last = nc.vector.scalar_tensor_tensor(out=pT[:, j], in0=adjT[i][:, j], scalar=0.0, in1=pT[:, j],
                                                          op0=ALU.is_gt if l == 0 else ALU.not_equal, op1=ALU.mult)
                last.then_inc(gat_probs[l].sem, 1)

            def gather(now, l, t):
                i = half_of(l)
                if l == 3 and t == 0:
                    stored.wait(dve, now.tail, 1)
                key = ("gat", l, t)
                bank = await_filled(dve, now, key)
                link(nc.vector.reciprocal(rcp[:, i, t:t + 1], bank[:, D:D + 1]))
                if l == 0:
                    nc.vector.tensor_scalar(elu_pos[:, t], bank[:, 0:D], rcp[:, i, t:t + 1], 0.0, ALU.mult, ALU.max)
                    nc.vector.tensor_scalar(elu_exp[:, t], bank[:, 0:D], rcp[:, i, t:t + 1], 0.0, ALU.mult,
                                            ALU.min).then_inc(emptied(now, key), 1)
                else:
                    nc.vector.scalar_tensor_tensor(out=result[:, t], in0=bank[:, 0:D], scalar=rcp[:, i, t:t + 1],
                                                   in1=xs[1][:, t], op0=ALU.mult,
                                                   op1=ALU.add).then_inc(emptied(now, key), 1)

            def elu(now):
                await_read(dve, now, [("gat", 0, t) for t in range(NT)])
                link(nc.vector.scalar_tensor_tensor(out=xs[0][:, :, :], in0=elu_pos[:, :, :], scalar=-1.0,
                                                    in1=x_new[:, :, :], op0=ALU.add, op1=ALU.add))
                dve.sem_inc(x_used.sem, 1)
                elu_out.wait(dve, now.front, 1)
                link(nc.vector.tensor_tensor(xs[0][:, :, :], xs[0][:, :, :], elu_exp[:, :, :], ALU.add))

            def output(now):
                bo_added.wait(dve, now.back, 1)
                for j in range(NT // 2):
                    key = ("wo", j)
                    bank = await_filled(dve, now, key)
                    last = nc.vector.tensor_tensor(xs[1][:, 2 * j:2 * j + 2], xs[0][:, 2 * j:2 * j + 2],
                                                   bank[:, :].rearrange("p (a d) -> p a d", a=2),
                                                   ALU.add)
                    last.then_inc(emptied(now, key), 1)

            masks_made = edge_masks_made = 0

            def one_pass(now):
                nonlocal links, masks_made, edge_masks_made
                links = 0
                dve.sem_clear(dve_chain)
                for name, arg in now.steps():
                    if name == "norm":
                        if arg == 0:
                            x_in.wait(dve, now.front, 16)
                        if arg == 2:
                            await_read(dve, now, [("wo", j) for j in range(NT // 2)])
                        if arg == 3:
                            await_read(dve, now, [("emix", t) for t in range(NT)])
                        statistics(now, arg)
                    if name == "turn":
                        i, key = half_of(arg), ("hT", arg, 0)
                        bank = await_filled(dve, now, key)
                        nc.vector.tensor_copy(hT[i][:, 0], bank[:, :]).then_inc(emptied(now, key), 1)
                    if name == "target":
                        target_terms(now, arg)
                    if name == "z":
                        target_maxima(now, arg)
                    if name == "weigh":
                        weigh(now, arg)
                    if name == "adj_apply":
                        adj_apply(now, arg)
                    if name == "gather":
                        gather(now, *divmod(arg, NT))
                    if name == "elu":
                        elu(now)
                    if name == "qk":
                        hi_ready.wait(dve, now.front, arg + 1)
                        key = ("qk", arg)
                        nc.vector.scalar_tensor_tensor(out=lo[:, arg], in0=place[now.part, key][0].tensor[:, :],
                                                       scalar=qk_bias[:, arg:arg + 1], in1=hi[:, arg], op0=ALU.add,
                                                       op1=ALU.subtract).then_inc(emptied(now, key), 1)
                    if name == "v":
                        key = ("v", arg)
                        bank = await_filled(dve, now, key)
                        nc.vector.tensor_tensor(values[:, 2 * arg:2 * arg + 2],
                                                bank[:, :].rearrange("p (a d) -> p a d", a=2),
                                                bv_bc[:, :].unsqueeze(1).to_broadcast([P, 2, D]),
                                                ALU.add).then_inc(emptied(now, key), 1)
                    if name == "masks":
                        adj_ready.wait(dve, now.front, 1)
                        nc.vector.tensor_scalar(mask[0][:, :, :], adjc[0][:, :, :], 0.0, MASKED, ALU.is_equal, ALU.mult)
                        link(nc.vector.tensor_scalar(maskT[:, :, :], adjT[0][:, :, :], 0.0, MASKED, ALU.is_equal,
                                                     ALU.mult))
                        masks_made = links
                        await_read(dve, now, [("v", j) for j in range(NT // 2)])
                        dve.sem_inc(attend_ready.sem, 1)
                    if name == "rowmax":
                        for head, t in half_head(arg):
                            key = ("scores", head, t)
                            bank = await_chain_and_filled(dve, now, key, masks_made)
                            nc.vector.tensor_tensor_reduce(out=elu_exp[:, t].bitcast(BF16), in0=bank[:, :], in1=mask[0][:, t], scale=1.0,
                                                           scalar=LOWEST, op0=ALU.add, op1=ALU.max,
                                                           accum_out=rowmax[:, head * NT + t:head * NT + t + 1]
                                                           ).then_inc(emptied(now, key), 1)
                    if name == "divide":
                        gr = arg
                        key = ("dens", gr)
                        bank = await_filled(dve, now, key)
                        nc.vector.reciprocal(rden[:, :], bank[:, :]).then_inc(emptied(now, key), 1)
                        await_read(dve, now, [key])
                        key = ("heads", gr)
                        bank = await_filled(dve, now, key)
                        nc.vector.tensor_tensor(heads[:, gr], bank[:, :], rden[:, :],
                                                ALU.mult).then_inc(emptied(now, key), 1)
                        await_read(dve, now, [key])
                        dve.sem_inc(heads_ready.sem, 1)
                    if name == "output":
                        output(now)
                    if name == "copy_adjacency":
                        if arg == 0 and now.part != FIRST:
                            await_read(dve, now, [("edge", 0)])
                        if arg == 1 and now.tail is not None:
                            gat_probs[3].wait(dve, now.tail, 1)
                        nc.vector.tensor_copy((adjc, adjT)[arg][1][:, :, :], (adjc, adjT)[arg][0][:, :, :]
                                              ).then_inc((adj_used, adjT_used)[arg].sem, 1)
                    if name == "edge_mask":
                        adj_used.wait(dve, now.back, 1 + 1)
                        edge_cleared.wait(dve, now.back, 1)
                        link(type_mask(0))
                        edge_masks_made = links
                    if name == "edge":
                        bank = await_chain_and_filled(dve, now, ("edge", arg), edge_masks_made)
                        take_scores(arg, bank).then_inc(emptied(now, ("edge", arg)), 1)
                    if name == "edge_rest":
                        with dve.If(types_beyond_one(dve, now) > 0):
                            await_read(dve, now, [("edge", t) for t in range(NT)])
                            for c in range(1, EDGE_TYPES):
                                if c > 1:
                                    dve.wait_ge(rest_read, (c - 1) * NT)
                                type_mask(c).then_inc(rest_chain, 1)
                                for t in range(NT):
                                    n = (c - 1) * NT + t
                                    dve.wait_ge(rest_chain, c)
                                    dve.wait_ge(rest_filled, n + 1)
                                    take_scores(t, rest_bank(n).tensor).then_inc(rest_read, 1)
                            nc.vector.memset(settled[:, :], 0.0).then_inc(rest_chain, 1)
                            dve.wait_ge(rest_chain, EDGE_TYPES)
                            dve.sem_clear(rest_chain)
                            dve.sem_clear(rest_filled)
                    if name == "edge_softmax":
                        await_read(dve, now, [("edge", t) for t in range(NT)])
                        link(nc.vector.reduce_max(edge_max[:, :], edge[:, :, :], AX))
                        link(nc.vector.scalar_tensor_tensor(out=edge_neg[:, :], in0=edge_max[:, :], scalar=SLOPE,
                                                            in1=edge_max[:, :], op0=ALU.mult, op1=ALU.max))
                        link(nc.vector.tensor_scalar(edge_neg[:, :], edge_neg[:, :], -1.0, None, ALU.mult))
                        nc.vector.scalar_tensor_tensor(out=edge[:, :, :], in0=edge[:, :, :], scalar=SLOPE,
                                                       in1=edge[:, :, :], op0=ALU.mult,
                                                       op1=ALU.max).then_inc(edge_ready.sem, 1)
                    if name == "edge_turn":
                        for j in range(0, NT, 2):
                            key = ("eprobs", j)
                            bank = await_filled(dve, now, key)
                            nc.vector.tensor_copy(back_probs[:, j], bank[:, :]).then_inc(emptied(now, key), 1)
                    if name == "edge_gather":
                        if arg == 0:
                            edge_probs.wait(dve, now.back, 1)
                            link(nc.vector.reciprocal(rcp[:, 1], edge_den[:, :]))
                        t, key = arg, ("emix", arg)
                        bank = await_filled(dve, now, key)
                        nc.vector.scalar_tensor_tensor(out=xs[1][:, t], in0=bank[:, 0:D], scalar=rcp[:, 1, t:t + 1],
                                                       in1=xs[1][:, t], op0=ALU.mult,
                                                       op1=ALU.add).then_inc(emptied(now, key), 1)

            run(dve, one_pass)

        @block.tensor
        def _(pe):
            pe.wait_ge(consts_in, CONST_DMAS * 16)
            pe.wait_ge(consts_made, POOL_CONSTS)
            for k in range(5):
                for c in range(DC):
                    n = k * DC + c
                    if n >= 2:
                        pe.wait_ge(setup_emptied, n - 1)
                    for r in range(DC):
                        last = nc.tensor.transpose(banks[n % 2].tensor[:, r * P:(r + 1) * P],
                                                   raw_weight(k)[:, r, c * P:(c + 1) * P], ident[:, :])
                    last.then_inc(setup_filled, 1)
            pe.wait_ge(setup_done, 2)

            def turn(now, key, src):
                bank = await_empty(pe, now, key)
                for t in range(NT):
                    last = nc.tensor.transpose(bank[:, t * P:(t + 1) * P], src(t), ident[:, :])
                last.then_inc(filled(now, key), 1)

            def products(bank, width, terms):
                for a, sums in enumerate(terms):
                    for n, (lhsT, rhs) in enumerate(sums):
                        last = nc.tensor.matmul(bank[:, a * width:(a + 1) * width], lhsT, rhs,
                                                start=(n == 0), stop=(n == len(sums) - 1))
                return last

            def product(now, key, width, terms):
                bank = await_empty(pe, now, key)
                products(bank, width, terms).then_inc(filled(now, key), 1)

            def edge_terms(c, t):
                return [[(ha[:, c % 2, k, t * P:(t + 1) * P], hT[1][:, k]) for k in range(DC)]]

            def project_nodes(now, key, nodesT, j, w):
                product(now, key, D, [[(nodesT[:, k, t * P:(t + 1) * P], w[:, k]) for k in range(DC)]
                                      for t in (2 * j, 2 * j + 1)])

            def mix(now, arg):
                gr, q = divmod(arg, NT)
                await_read(pe, now, [("turned", arg, hh) for hh in range(HPG)])
                if q == 0 and (gr or now.part != FIRST):
                    last_group = (gr - 1) % GROUPS
                    await_read(pe, now, [("heads", last_group), ("dens", last_group)])
                for key, ring in ((("heads", gr), "mixed"), (("dens", gr), "dens")):
                    bank = banks[RINGS[ring][0]].tensor
                    for hh in range(HPG):
                        e = (gr * HPG + hh) * HD
                        weights = values[:, q, e:e + HD] if key[0] == "heads" else ones[:, 0:HD]
                        last = nc.tensor.matmul(bank[hh * HD:(hh + 1) * HD, :], weights, attend_probs[:, arg % 2, hh],
                                                start=(q == 0), stop=(q == NT - 1))
                    if q == NT - 1:
                        last.then_inc(filled(now, key), 1)

            def one_pass(now):
                for name, arg in now.steps():
                    if name == "norm":
                        pass
                    if name == "turn":
                        i = half_of(arg)
                        h_ready[arg].wait(pe, now.graph, 1)
                        for k in range(DC):
                            turn(now, ("hT", arg, k), lambda q: hs[i][:, q, k * P:(k + 1) * P])
                    if name == "project":
                        i = half_of(arg)
                        await_read(pe, now, hT_keys(arg))
                        for j in range(NT // 2):
                            project_nodes(now, ("wh", arg, j), hT[i], j, (w0, w3T)[i])
                        product(now, ("f", arg), N, [[(f_rep[:, i, k], hT[i][:, k]) for k in range(DC)]])
                    if name == "adjacency":
                        adj_ready.wait(pe, now.front, 1)
                        for j in range(NT // 2):
                            key = ("adj", j)
                            bank = await_empty(pe, now, key)[:, :].bitcast(BF16)
                            for a in range(2):
                                for t in range(NT):
                                    last = nc.tensor.transpose(bank[:, a * N + t * P:a * N + (t + 1) * P],
                                                               adjc[0][:, t, (2 * j + a) * P:(2 * j + a + 1) * P],
                                                               identb[:, :])
                            last.then_inc(filled(now, key), 1)
                    if name == "gather":
                        l, t = divmod(arg, NT)
                        i = half_of(l)
                        if t == 0:
                            gat_probs[l].wait(pe, now.graph, 1)
                        product(now, ("gat", l, t), D + 1,
                                [[(gat_pT[i][:, j, t * P:(t + 1) * P], wh[i][:, j]) for j in range(NT)]])
                    if name == "qk":
                        if arg == 0:
                            await_read(pe, now, hT_keys(1))
                        gr, keys = divmod(arg, 2)
                        product(now, ("qk", arg), N, [[((wqT, wkT)[keys][:, k, gr * P:(gr + 1) * P], hT[0][:, k])
                                                       for k in range(DC)]])
                    if name == "v":
                        project_nodes(now, ("v", arg), hT[0], arg, wvT)
                    if name == "rowmax":
                        if arg % (2 * HPG) == 0:
                            stacked[arg // (2 * HPG)].wait(pe, now.front, STACK_DMAS * 16)
                        for head, t in half_head(arg):
                            product(now, ("scores", head, t), N,
                                    [[(qs[0:SPLIT_ROWS, head, t * P:(t + 1) * P], ks[0:SPLIT_ROWS, head])]])
                    if name == "shift":
                        await_read(pe, now, [("scores", (arg + 1) * HPG - 1, t) for t in range(NT)])
                        key = ("shift", arg)
                        bank = await_empty(pe, now, key)
                        nc.tensor.transpose(bank[0:HPG * NT, 0:P], rowmax[:, arg * HPG * NT:(arg + 1) * HPG * NT],
                                            ident[:, :]).then_inc(filled(now, key), 1)
                    if name == "attend":
                        if arg == 0:
                            attend_ready.wait(pe, now.front, 1)
                            pe.wait_ge(consts_made, POOL_CONSTS)
                        gr, q = divmod(arg, NT)
                        if q == 0:
                            shift_in[gr].wait(pe, (now.front, now.back)[gr], 16)
                        for hh in range(HPG):
                            head = gr * HPG + hh
                            product(now, ("turned", arg, hh), N,
                                    [[(ks[:, head, q * P:(q + 1) * P], qs[:, head]), (identb[:, :], maskT[:, q])]])
                    if name == "mix":
                        mix(now, arg)
                    if name == "output":
                        heads_ready.wait(pe, now.back, GROUPS)
                        for j in range(NT // 2):
                            project_nodes(now, ("wo", j), heads, j, woT)
                    if name == "edge":
                        if arg == 0:
                            await_read(pe, now, hT_keys(2))
                            ha_ready.wait(pe, now.back, 1)
                        product(now, ("edge", arg), N, edge_terms(0, arg))
                    if name == "edge_rest":
                        with pe.If(types_beyond_one(pe, now) > 0):
                            await_read(pe, now, [("edge", t) for t in range(NT)])
                            for c in range(1, EDGE_TYPES):
                                pe.wait_ge(rest_scaled, c)
                                for t in range(NT):
                                    n = (c - 1) * NT + t
                                    if n >= len(RINGS["back"]):
                                        pe.wait_ge(rest_read, n + 1 - len(RINGS["back"]))
                                    products(rest_bank(n).tensor, N, edge_terms(c, t)).then_inc(rest_filled, 1)
                            pe.wait_ge(rest_read, (EDGE_TYPES - 1) * NT)
                            pe.sem_clear(rest_scaled)
                            pe.sem_clear(rest_read)
                    if name == "edge_turn":
                        edge_probs.wait(pe, now.back, 1)
                        for j in range(NT):
                            turn(now, ("eprobs", j), lambda q: edge[:, q, j * P:(j + 1) * P])
                    if name == "edge_gather":
                        t = arg
                        if arg == 0:
                            await_read(pe, now, [("eprobs", j) for j in range(NT)])
                        product(now, ("emix", t), D,
                                [[(back_probs[:, j, t * P:(t + 1) * P], hs[1][:, j]) for j in range(NT)]])

            for bank in banks:
                pe.sem_inc(bank.emptied, 1)
            run(pe, one_pass)


_INS = ["x", "adj", "L0_gnn_W", "L0_gnn_a", "L1_gnn_Wq", "L1_gnn_bq", "L1_gnn_Wk", "L1_gnn_bk", "L1_gnn_Wv", "L1_gnn_bv",
        "L1_gnn_Wo", "L1_gnn_bo", "L2_gnn_a0", "L2_gnn_a1", "L2_gnn_a2", "L2_gnn_a3", "L3_gnn_W", "L3_gnn_a"]


def kernel(**inputs):
    import numpy as np
    import concourse.bacc as bacc
    from concourse.bass_utils import run_bass_kernel_spmd

    nc = bacc.Bacc("TRN2", target_bir_lowering=False, num_devices=1)
    arrays, args = {}, []
    for name in _INS:
        a = np.ascontiguousarray(inputs[name])
        if a.shape[:1] == (1,):
            a = a.reshape(-1)
        arrays[f"in_{name}"] = a
        args.append(nc.dram_tensor(f"in_{name}", a.shape, mybir.dt.from_np(a.dtype), kind="ExternalInput").ap())
    out = nc.dram_tensor("out", inputs["x"].shape, F32, kind="ExternalOutput").ap()
    gnn_stack_kernel(nc, *args, out)
    result = run_bass_kernel_spmd(nc, [arrays], core_ids=[0])
    return result.results[0]["out"]
```
